# Optimizing a Trainium2 kernel written in Bass

```python
import numpy as np
import jax
import jax.numpy as jnp

def _softmax(x, axis=-1):
    return jax.nn.softmax(x, axis=axis)

def _gelu(x):
    return jax.nn.gelu(x, approximate=True)

def _silu(x):
    return jax.nn.silu(x)

def _sigmoid(x):
    return jax.nn.sigmoid(x)

def _layernorm(x, axis=-1, eps=1e-05):
    m = jnp.mean(x, axis=axis, keepdims=True)
    v = jnp.var(x, axis=axis, keepdims=True)
    return (x - m) / jnp.sqrt(v + eps)

def _scatter_add(tgt, idx, src, axis=0):
    return tgt.at[idx].add(src)

def _segment_sum(src, seg, n):
    return jax.ops.segment_sum(src, seg, n)
kernel_name = 'mk_adaln_d1_jaxref_r4_1611ef'

def setup_inputs(seed: int=0):
    np.random.seed(seed)
    _w = jnp.asarray

    def _L0_attn_setup():
        import jax, jax.numpy as jnp
        import numpy as np
        N_HEADS = 16
        CHUNK = 128

        def _phi(x):
            return jax.nn.elu(x) + 1.0
        key = jax.random.key(seed)
        ks = jax.random.split(key, 5)
        d = 256
        scale = (2.0 / (d + d)) ** 0.5
        W = lambda k: jax.random.normal(k, (d, d), jnp.float32) * scale
        return {'x': jax.random.normal(ks[0], (4, 1024, d), jnp.float32), 'Wq': W(ks[1]), 'bq': jnp.zeros((d,), jnp.float32), 'Wk': W(ks[2]), 'bk': jnp.zeros((d,), jnp.float32), 'Wv': W(ks[3]), 'bv': jnp.zeros((d,), jnp.float32), 'Wo': W(ks[4]), 'bo': jnp.zeros((d,), jnp.float32)}
    _L0_attn_in = _L0_attn_setup()

    def _L0_ffn_setup():
        import jax, jax.numpy as jnp
        import numpy as np
        import math
        B, S, H = (8, 1024, 256)
        E, I, K = (8, 512, 2)
        CAP_FACTOR = 1.0

        def _router(x, expert_embeddings):
            dot = jnp.einsum('bsh,eh->bse', x, expert_embeddings)
            n = dot.shape[0] * dot.shape[1]
            dot2 = dot.reshape(n, E)
            vals, idx = jax.lax.top_k(dot2, K)
            rows = jnp.arange(n)[:, None]
            masked = jnp.full_like(dot2, -jnp.inf).at[rows, idx].set(vals)
            return jax.nn.softmax(masked, axis=-1)
        key = jax.random.key(seed)
        k1, k2, k3, k4 = jax.random.split(key, 4)

        def kaiming(k, shape):
            bound = math.sqrt(3.0 / shape[-1])
            return jax.random.uniform(k, shape, jnp.float32, -bound, bound)
        x = jax.random.normal(k1, (B, S, H), jnp.float32)
        expert_embeddings = kaiming(k2, (E, H))
        first_linear = kaiming(k3, (E, I, H))
        second_linear = kaiming(k4, (E, H, I))
        return {'x': x, 'expert_embeddings': expert_embeddings, 'first_linear': first_linear, 'second_linear': second_linear}
    _L0_ffn_in = _L0_ffn_setup()
    _L0_c = _w((lambda *s: np.random.randn(*s).astype(np.float32) * 0.05)(8, 256))
    _L0_wmod = _w((lambda *s: np.random.randn(*s).astype(np.float32) * 0.05)(256, 6 * 256) * 256 ** (-0.5))
    _d = {'L0_attn_x': _L0_attn_in['x'], 'L0_attn_Wq': _L0_attn_in['Wq'], 'L0_attn_bq': _L0_attn_in['bq'], 'L0_attn_Wk': _L0_attn_in['Wk'], 'L0_attn_bk': _L0_attn_in['bk'], 'L0_attn_Wv': _L0_attn_in['Wv'], 'L0_attn_bv': _L0_attn_in['bv'], 'L0_attn_Wo': _L0_attn_in['Wo'], 'L0_attn_bo': _L0_attn_in['bo'], 'L0_ffn_expert_embeddings': _L0_ffn_in['expert_embeddings'], 'L0_ffn_first_linear': _L0_ffn_in['first_linear'], 'L0_ffn_second_linear': _L0_ffn_in['second_linear'], 'L0_c': _L0_c, 'L0_wmod': _L0_wmod}
    _x0 = _d['L0_attn_x']
    _d['L0_attn_x'] = jax.random.normal(jax.random.fold_in(jax.random.key(seed), 1), (8, 512, 256), dtype=_x0.dtype)
    del _x0
    return _d

def reference(L0_attn_x, L0_attn_Wq, L0_attn_bq, L0_attn_Wk, L0_attn_bk, L0_attn_Wv, L0_attn_bv, L0_attn_Wo, L0_attn_bo, L0_ffn_expert_embeddings, L0_ffn_first_linear, L0_ffn_second_linear, L0_c, L0_wmod):

    def _L0_attn_ref(x, Wq, bq, Wk, bk, Wv, bv, Wo, bo):
        import jax, jax.numpy as jnp
        import numpy as np
        N_HEADS = 16
        CHUNK = 128

        def _phi(x):
            return jax.nn.elu(x) + 1.0
        b, s, dm = x.shape
        h = N_HEADS
        d = dm // h

        def proj(W, bias):
            y = x @ W.T + bias
            return y.reshape(b, s, h, d).transpose(0, 2, 1, 3).reshape(b * h, s, d)
        q = _phi(proj(Wq, bq))
        k = _phi(proj(Wk, bk))
        v = proj(Wv, bv)
        C = CHUNK
        n = s // C
        to_chunks = lambda t: t.reshape(b * h, n, C, d).transpose(1, 0, 2, 3)
        qc, kc, vc = (to_chunks(q), to_chunks(k), to_chunks(v))
        mask = jnp.tril(jnp.ones((C, C), bool))

        def step(carry, inp):
            S, z = carry
            qi, ki, vi = inp
            scores = jnp.einsum('bqd,bkd->bqk', qi, ki)
            scores = jnp.where(mask, scores, jnp.zeros((), scores.dtype))
            num = jnp.einsum('bqk,bkd->bqd', scores, vi) + jnp.einsum('bqd,bde->bqe', qi, S)
            kcum = jnp.cumsum(ki, axis=1) + z[:, None, :]
            den = jnp.sum(qi * kcum, axis=-1, keepdims=True)
            out = num / den
            S2 = S + jnp.einsum('bkd,bke->bde', ki, vi)
            z2 = z + ki.sum(axis=1)
            return ((S2, z2), out)
        init = (jnp.zeros((b * h, d, d), x.dtype), jnp.zeros((b * h, d), x.dtype))
        _, outs = jax.lax.scan(step, init, (qc, kc, vc))
        out = outs.transpose(1, 0, 2, 3).reshape(b, h, s, d).transpose(0, 2, 1, 3).reshape(b, s, dm)
        return out @ Wo.T + bo

    def _L0_ffn_ref(x, expert_embeddings, first_linear, second_linear):
        import jax, jax.numpy as jnp
        import numpy as np
        import math
        B, S, H = (8, 1024, 256)
        E, I, K = (8, 512, 2)
        CAP_FACTOR = 1.0

        def _router(x, expert_embeddings):
            dot = jnp.einsum('bsh,eh->bse', x, expert_embeddings)
            n = dot.shape[0] * dot.shape[1]
            dot2 = dot.reshape(n, E)
            vals, idx = jax.lax.top_k(dot2, K)
            rows = jnp.arange(n)[:, None]
            masked = jnp.full_like(dot2, -jnp.inf).at[rows, idx].set(vals)
            return jax.nn.softmax(masked, axis=-1)
        batch, seq, hidden = x.shape
        n_tokens = batch * seq
        expert_capacity = math.ceil(n_tokens / E * CAP_FACTOR)
        weights = _router(x, expert_embeddings)
        ones = (weights > 0).astype(weights.dtype)
        cap_ones = jnp.where(jnp.cumsum(ones, axis=0) <= expert_capacity, ones, 0.0)
        caw = weights * cap_ones
        vals, idx = jax.lax.top_k(caw.T, expert_capacity)
        index = idx.reshape(-1)
        x_flat = x.reshape(n_tokens, hidden)
        tokens = x_flat[index].reshape(E, expert_capacity, hidden)
        inter = jax.nn.relu(jnp.einsum('ech,eih->eci', tokens, first_linear))
        out = jnp.einsum('eci,ehi->ech', inter, second_linear)
        out = out * vals[:, :, None]
        final = jnp.zeros((n_tokens, hidden), x.dtype).at[index].add(out.reshape(-1, hidden))
        return final.reshape(x.shape)
    x = L0_attn_x
    mod = (_silu(L0_c) @ L0_wmod).reshape(L0_c.shape[0], 6, 1, -1)
    sa, ca, ga, sb, cb, gb = (mod[:, 0], mod[:, 1], mod[:, 2], mod[:, 3], mod[:, 4], mod[:, 5])
    ga = (2 * (ga >= 0) - 1) * jnp.maximum(jnp.abs(ga), 0.25)
    gb = (2 * (gb >= 0) - 1) * jnp.maximum(jnp.abs(gb), 0.25)
    h = _layernorm(x, axis=-1) * (1 + ca) + sa
    x = x + ga * _L0_attn_ref(h, L0_attn_Wq, L0_attn_bq, L0_attn_Wk, L0_attn_bk, L0_attn_Wv, L0_attn_bv, L0_attn_Wo, L0_attn_bo)
    h = _layernorm(x, axis=-1) * (1 + cb) + sb
    x = x + gb * _L0_ffn_ref(h, L0_ffn_expert_embeddings, L0_ffn_first_linear, L0_ffn_second_linear)
    return x

_drawn_inputs = setup_inputs


def setup_inputs(seed=0):
    import zlib

    import numpy as np

    out = dict(_drawn_inputs(seed))
    spreads = {'L0_attn_bq': (0.0, 2.0),
     'L0_attn_bk': (0.0, 2.0),
     'L0_attn_bv': (0.0, 0.273),
     'L0_attn_bo': (0.0, 0.279)}
    factors = {'L0_attn_Wq': 103.369, 'L0_attn_Wk': 49.425}
    for name, (base, spread) in spreads.items():
        noise = np.random.default_rng([zlib.crc32(name.encode()), seed]).standard_normal(out[name].shape)
        drawn = base * np.exp(spread * noise) if base else spread * noise
        out[name] = jnp.asarray(drawn.astype(out[name].dtype))
    for name, factor in factors.items():
        out[name] = (out[name] * factor).astype(out[name].dtype)
    return out
```

```python
from collections import namedtuple
from contextlib import ExitStack

import concourse.bass as bass
from concourse import mybir

F32 = mybir.dt.float32
BF16 = mybir.dt.bfloat16
I32 = mybir.dt.int32
U32 = mybir.dt.uint32
ALU = mybir.AluOpType
ACT = mybir.ActivationFunctionType
AX = mybir.AxisListType

P = 128
BATCH, SEQ, D = 8, 512, 256
HEADS, HD = 16, 16
KH = D // P
TILES = SEQ // P
HPH = P // HD
QUADS = HEADS // 4
TOKENS = BATCH * SEQ
EXPERTS, INTER = 8, 512
CAP = -(-TOKENS // EXPERTS)
SLOT_TILES = CAP // P
LISTS = EXPERTS * SLOT_TILES
IB = INTER // P
EPS = 1e-5
NO_SLOT = 2 * EXPERTS * CAP - 1
ROW_W, ROW_G = D, D + EXPERTS
ROW = 2 * D + EXPERTS
MODS = 6
SA, CA, GA, SB, CB, GB = range(MODS)

Batch = namedtuple("Batch", "n h p")


def batch(h, p):
    return Batch(2 * h + p, h, p)


def wait(eng, sem, value):
    if isinstance(value, int) and value <= 0:
        return
    eng.wait_ge(sem, value)


def steps(eng, step):
    last = BATCH // 2
    step(batch(0, 0), None, None, None)
    step(batch(0, 1), batch(0, 0), None, None)
    step(batch(1, 0), batch(0, 1), batch(0, 0), None)
    step(batch(1, 1), batch(1, 0), batch(0, 1), batch(0, 0))
    with eng.Fori(1, last - 1) as i:
        step(batch(i + 1, 0), batch(i, 1), batch(i, 0), batch(i - 1, 1))
        step(batch(i + 1, 1), batch(i + 1, 0), batch(i, 1), batch(i, 0))
    step(None, batch(last - 1, 1), batch(last - 1, 0), batch(last - 2, 1))
    step(None, None, batch(last - 1, 1), batch(last - 1, 0))
    step(None, None, None, batch(last - 1, 1))


def adaln_kernel(nc, x, wqT, wkT, wvT, woT, biases, bo, embT, w1T, w2T, cT, wmod, out):
    rows = nc.dram_tensor("token_rows", (TOKENS, ROW), F32, kind="Internal").ap()
    den_dram = nc.dram_tensor("den_rows", (BATCH, HEADS, SEQ), F32, kind="Internal").ap()
    rden_dram = nc.dram_tensor("rden_rows", (BATCH, HEADS, SEQ), F32, kind="Internal").ap()
    mod_dram = nc.dram_tensor("mod_rows", (BATCH, MODS * D), F32, kind="Internal").ap()
    x_tiles = x.rearrange("b (t p) d -> b p t d", p=P)
    out_rows = out.rearrange("b s d -> (b s) d")
    out_tiles = out.rearrange("b (t p) d -> b p t d", p=P)
    row_tiles = rows.rearrange("(b t p) r -> b p t r", p=P, t=TILES)

    ctx = ExitStack()
    with ctx:
        def sb(name, shape, dt=F32):
            return ctx.enter_context(nc.sbuf_tensor(name, shape, dt))

        def sem(name):
            return ctx.enter_context(nc.semaphore(name))

        wq_sb, wk_sb, wv_sb, wo_sb = (sb(f"w{c}_sb", [P, KH, D]) for c in "qkvo")
        emb_sb = sb("emb_sb", [P, KH, EXPERTS])
        bias_in = sb("bias_in", [P, 3, KH])
        bias_p1 = sb("bias_p1", [P, 2, KH])
        neg_bk = sb("neg_bk", [P, KH])
        bo_row = sb("bo_row", [1, D])
        ident = sb("ident", [P, P])
        same_head = sb("same_head", [P, P])
        head_sum = sb("head_sum", [P, KH, HEADS])
        causal = sb("causal", [P, P])
        causal_bf = sb("causal_bf", [P, P], BF16)
        ones = sb("ones", [P, SEQ])
        ones_bf = sb("ones_bf", [P, P], BF16)
        neg_half = sb("neg_half", [P, TILES])
        iota_p = sb("iota_p", [P, 1])
        iota_128 = sb("iota_128", [P, P], BF16)
        iota_list = sb("iota_list", [P, LISTS])
        iota_exp = sb("iota_exp", [P, EXPERTS])
        slot_base = sb("slot_base", [P, EXPERTS])
        tile_no = sb("tile_no", [P, TILES, 2])
        spare = sb("spare", [P, 64])
        c_sb = sb("c_sb", [P, KH, BATCH])
        c_exp = sb("c_exp", [P, KH, BATCH])
        silu = sb("silu", [P, KH, BATCH])
        mod_T = sb("mod_T", [P, 2, KH, BATCH])
        bo_all = sb("bo_all", [P, D])
        ga_all = [sb(f"ga_all{p}", [P, D]) for p in range(2)]
        mod_all = [sb(f"mod_all{p}", [P, 3, D]) for p in range(2)]
        x_sb = [sb(f"x_sb{p}", [P, TILES, D]) for p in range(2)]
        stat1 = sb("stat1", [P, TILES, 6])
        mv1 = sb("mv1", [P, TILES, 2])
        rstd1 = sb("rstd1", [P, TILES])
        var1 = sb("var1", [P, TILES])
        negm1 = sb("negm1", [P, TILES])
        xn = sb("xn", [P, TILES, D])
        h1T = sb("h1T", [P, KH, SEQ])
        q_exp = sb("q_exp", [P, KH, SEQ])
        k_exp = sb("k_exp", [P, KH, SEQ])
        kcum = sb("kcum", [P, KH, SEQ])
        qk = kcum
        den_sb = k_exp[0:HEADS, 0, :]
        den_flat = sb("den_flat", [P, HEADS * SEQ // P])
        rden_flat = sb("rden_flat", [P, HEADS * SEQ // P])
        rden = [sb(f"rden{p}", [P, KH, SEQ]) for p in range(2)]
        qT = [sb(f"qT{p}", [P, KH, SEQ]) for p in range(2)]
        kT = [sb(f"kT{p}", [P, KH, SEQ]) for p in range(2)]
        k_tok = [sb(f"k_tok{p}", [P, TILES - 1, D]) for p in range(2)]
        v_pad = [sb(f"v_pad{p}", [P, TILES, HEADS // 2, 4, HD]) for p in range(2)]
        q_wide = [sb(f"q_wide{p}", [P, KH, HPH, SEQ]) for p in range(2)]
        sT = [sb(f"sT{r}", [P, HEADS, P]) for r in range(2)]
        state = [sb(f"state{r}", [P, KH, P]) for r in range(2)]
        oT = [sb(f"oT{r}", [P, KH, P]) for r in range(2)]
        wog = sb("wog", [P, KH, D])
        bo_g = sb("bo_g", [P, D])
        x1 = [sb(f"x1_{p}", [P, TILES, D]) for p in range(2)]
        stat2 = sb("stat2", [P, TILES, 6])
        mv2 = sb("mv2", [P, TILES, 2])
        var2 = sb("var2", [P, TILES])
        rstd2 = sb("rstd2", [P, TILES])
        h2 = sb("h2", [P, TILES, D + EXPERTS])
        h2T = sb("h2T", [P, KH, SEQ])
        logits = sb("logits", [P, TILES, EXPERTS])
        top = sb("top", [P, TILES, 8])
        top_i = sb("top_i", [P, TILES, 8], U32)
        top_f = sb("top_f", [P, TILES, 2])
        gap = sb("gap", [P, TILES])
        e2 = sb("e2", [P, TILES])
        w12 = sb("w12", [P, 2, TILES])
        wsum = sb("wsum", [P, TILES])
        alive = sb("alive", [P, TILES])
        one_hot = sb("one_hot", [P, 2, TILES, EXPERTS])
        weighted = sb("weighted", [P, 2, TILES, EXPERTS])
        both_bf = sb("both_bf", [P, TILES, EXPERTS], BF16)
        counts = sb("counts", [P, TILES + 1, EXPERTS])
        counts_bf = sb("counts_bf", [P, TILES, EXPERTS], BF16)
        fits = sb("fits", [P, TILES, EXPERTS])
        slot = sb("slot", [P, TILES, EXPERTS])
        chosen = sb("chosen", [P, 2, TILES, EXPERTS])
        slot_f = sb("slot_f", [P, TILES, 2])
        slot_i = sb("slot_i", [P, TILES, 2], I32)
        part_i = sb("part_i", [P, 2, TILES, 2], I32)
        part_f = sb("part_f", [P, 2, TILES, 2])
        in_list = sb("in_list", [P, 2 * TILES, 3, LISTS], BF16)
        in_slot = sb("in_slot", [P, 2 * TILES, P], BF16)
        lists = sb("lists", [P, 3, LISTS])
        tok_f = den_flat[:, 0:2 * LISTS].rearrange("p (a l) -> p a l", a=2)
        tok_i = sb("tok_i", [P, 2, LISTS], I32)
        list_in = [sb(f"list_in{q}", [P, SLOT_TILES], I32) for q in range(2)]
        list_back = [sb(f"list_back{q}", [P, SLOT_TILES], I32) for q in range(2)]
        w_now = [sb(f"w_now{q}", [P, SLOT_TILES]) for q in range(2)]

        def carve(p):
            flat = q_wide[p][:, :, :, :].rearrange("p a b c -> p (a b c)")
            at = [0]

            def take(n):
                at[0] += n
                return flat[:, at[0] - n:at[0]]
            return (take(SLOT_TILES * ROW).rearrange("p (t r) -> p t r", r=ROW),
                    take(SLOT_TILES * (EXPERTS + D)).rearrange("p (t r) -> p t r", r=EXPERTS + D),
                    take(KH * CAP).rearrange("p (k c) -> p k c", k=KH),
                    take(KH * INTER).rearrange("p (k i) -> p k i", k=KH),
                    take(IB * D).rearrange("p (k d) -> p k d", k=IB))
        (xg, aside, xgT, w1_sb, w2_sb) = zip(carve(0), carve(1))
        inner = [sT[q][:, :, :].rearrange("p a b -> p (a b)").rearrange("p (i c) -> p i c", i=IB)
                 for q in range(2)]
        y_sb = x1
        wmod_sb = [qT[0], qT[1], kT[0]]

        flat = [sT[r][0:BATCH, :, :].rearrange("b h i -> b (h i)") for r in range(2)]
        mod_sb = flat[0][:, 0:MODS * D].rearrange("b (m d) -> b m d", m=MODS)
        mod_abs = flat[1][:, 0:2 * D].rearrange("b (m d) -> b m d", m=2)
        mod_sign = flat[1][:, 2 * D:4 * D].rearrange("b (m d) -> b m d", m=2)

        bv_wide = sT[1][:, HEADS - KH:HEADS, :]

        bank = [ctx.enter_context(nc.psum_tensor(f"bank{i}", [P, 512], F32)) for i in range(8)]
        ring = bank[0:2]
        sc_bank = bank[2:4]
        oT_bank, kv_bank, wo_bank, rt_bank = bank[4:8]

        names = """
            w_in c_in mod_out ident_on mask_on const_on zero_q0 zero_q1 zero_v c_neg silu_on mod_mm
            mod_ev gate_on mod_t modT_on bias_on bvw_on bo_mm bo_on
            stats1 mean1 rstd1_on xn_on pe_front h1T_on q_min q_expd q_on k_expd k_on v_on k_tok_on
            kcum_on qk_on den_on rden_on head_on
            sc_on masked oT_mm oT_on kv_mm state_on wo_mm wog_on bog_on xb_on x1_on
            stats2 mean2 rstd2_on h2a_on h2_on pe_route h2T_on logits_on top_on topi_on gap_on e2_on
            small oh_on slots_on lists_on w8_on
            tok_on list_ld back_ld gT_mm xgT_on m1_mm relu_a relu_v aside_on w_ld m2_mm y_on scat
        """.split()
        S = {n: sem(n) for n in names}
        den_out, den_in, rden_out = sem("den_out"), sem("den_in"), sem("rden_out")
        rden_in = [sem(f"rden_in{p}") for p in range(2)]
        wmod_in = [sem(f"wmod_in{j}") for j in range(3)]
        x_in = [sem(f"x_in{p}") for p in range(2)]
        ga_in = [sem(f"ga_in{p}") for p in range(2)]
        mod_in = [sem(f"mod_in{p}") for p in range(2)]
        q_wide_in = [[sem(f"q_wide_in{p}{k}") for k in range(KH)] for p in range(2)]
        x1_out = [sem(f"x1_out{p}") for p in range(2)]
        rows_out = sem("rows_out")
        exp_w_in = [sem(f"exp_w_in{q}") for q in range(2)]
        gathered = [sem(f"gathered{q}") for q in range(2)]
        SMALL = 31

        held = [0]

        def hold(eng, sem, value):
            wait(eng, sem, value)
            if not isinstance(value, int):
                cell = spare[:, held[0]:held[0] + 1]
                held[0] += 1
                if eng is nc.gpsimd:
                    eng.tensor_tensor(cell, neg_half[:, 0:1], neg_half[:, 0:1], ALU.add)
                else:
                    eng.memset(cell, 0.0)

        block = ctx.enter_context(nc.Block())

        def tok(t):
            return slice(t * P, (t + 1) * P)

        def wide(ap, shape):
            return ap.to_broadcast(shape)

        @block.sync
        def _(sp):
            sp.dma_start(c_sb[:, :, :], cT.rearrange("(k p) b -> p k b", p=P)).then_inc(S["c_in"], 16)
            for j in range(3):
                sp.dma_start(wmod_sb[j][:, :, :],
                             wmod[:, j * 2 * D:(j + 1) * 2 * D].rearrange("(k p) m -> p k m", p=P))\
                    .then_inc(wmod_in[j], 16)

            def load_weights():
                loads = [(wq_sb, wqT), (wk_sb, wkT), (wv_sb, wvT), (wo_sb, woT), (emb_sb, embT)]
                for to, of in loads:
                    sp.dma_start(to[:, :, :], of.rearrange("(k p) m -> p k m", p=P)).then_inc(S["w_in"], 16)
                sp.dma_start(bias_in[:, :, :], biases).then_inc(S["w_in"], 16)
                sp.dma_start(bo_row[:, :], bo.rearrange("(a d) -> a d", a=1)).then_inc(S["w_in"], 16)

            def load_x(b):
                wait(sp, S["xb_on"], b.n - 1)
                sp.dma_start(x_sb[b.p][:, :, :], x_tiles[b.n]).then_inc(x_in[b.p], 16)

            def load_ga(b):
                wait(sp, S["wog_on"], KH * (b.n - 1))
                sp.dma_start(ga_all[b.p][:, :], mod_dram[b.n, GA * D:(GA + 1) * D].partition_broadcast(P))\
                    .then_inc(ga_in[b.p], 16)

            def load_mod(b):
                wait(sp, rows_out, 32 * (b.n - 1))
                sp.dma_start(mod_all[b.p][:, :, :].rearrange("p m d -> p (m d)"),
                             mod_dram[b.n, SB * D:MODS * D].partition_broadcast(P))\
                    .then_inc(mod_in[b.p], 16)

            def spread_q(b):
                wait(sp, S["sc_on"], TILES * QUADS * (b.n - 1))
                for k in range(KH):
                    wait(sp, S["q_on"], KH * b.n + k + 1)
                    for h in range(HPH):
                        at = slice(HD * h, HD * (h + 1))
                        sp.dma_start(q_wide[b.p][at, k, h, :], qT[b.p][at, k, :])\
                            .then_inc(q_wide_in[b.p][k], 16)

            def spread_den(b):
                wait(sp, S["den_on"], b.n + 1)
                sp.dma_start(den_dram[b.n], den_sb).then_inc(den_out, 16)
                wait(sp, den_out, 16 * (b.n + 1))
                wait(sp, S["rden_on"], b.n)
                sp.dma_start(den_flat[:, :], den_dram[b.n].rearrange("h (g t) -> (h g) t", g=P // HEADS))\
                    .then_inc(den_in, 16)

            def spread_rden(b):
                wait(sp, S["rden_on"], b.n + 1)
                sp.dma_start(rden_dram[b.n].rearrange("h (g t) -> (h g) t", g=P // HEADS), rden_flat[:, :])\
                    .then_inc(rden_out, 16)
                wait(sp, rden_out, 16 * (b.n + 1))
                for h in range(HPH):
                    sp.dma_start(rden[b.p][HD * h:HD * (h + 1), :, :],
                                 rden_dram[b.n, h:HEADS:HPH, :].partition_broadcast(HD))\
                        .then_inc(rden_in[b.p], 16)

            def step(early, front, attend, route):
                if attend:
                    spread_rden(attend)
                if early:
                    load_x(early)
                    if isinstance(early.n, int) and early.n == 0:
                        load_weights()
                if route:
                    wait(sp, S["x1_on"], TILES * (route.n + 1))
                    sp.dma_start(out_tiles[route.n], x1[route.p][:, :, :]).then_inc(x1_out[route.p], 16)
                if front:
                    if isinstance(front.n, int) and front.n == 0:
                        wait(sp, S["gate_on"], 4)
                        sp.dma_start(mod_dram, mod_sb[:, :, :].rearrange("b m d -> b (m d)"))\
                            .then_inc(S["mod_out"], 16)
                        wait(sp, S["mod_out"], 16)
                        wait(sp, S["zero_q0"], 1)
                    load_ga(front)
                    if isinstance(front.n, int) and front.n == 1:
                        wait(sp, S["zero_q1"], 1)
                    spread_q(front)
                if route:
                    wait(sp, S["w8_on"], route.n + 1)
                    sp.dma_start(row_tiles[route.n, :, :, 0:ROW_G], h2[:, :, :]).then_inc(rows_out, 16)
                    sp.dma_start(row_tiles[route.n, :, :, ROW_G:ROW],
                                 mod_all[route.p][:, 2, :].unsqueeze(1).to_broadcast([P, TILES, D]))\
                        .then_inc(rows_out, 16)
                if front:
                    load_mod(front)
                    spread_den(front)

            steps(sp, step)

            def load_expert(e, q):
                wait(sp, S["m2_mm"], SLOT_TILES * (e - 1))
                sp.dma_start(w1_sb[q][:, :, :], w1T[e].rearrange("(k p) i -> p k i", p=P))\
                    .then_inc(exp_w_in[q], 16)
                sp.dma_start(w2_sb[q][:, :, :], w2T[e].rearrange("(k p) d -> p k d", p=P))\
                    .then_inc(exp_w_in[q], 16)

            wait(sp, S["sc_on"], TILES * QUADS * BATCH)
            load_expert(0, 0)
            load_expert(1, 1)
            with sp.Fori(1, EXPERTS // 2) as i:
                load_expert(2 * i, 0)
                load_expert(2 * i + 1, 1)
            wait(sp, S["scat"], 16 * LISTS)
            for p in range(2):
                wait(sp, x1_out[p], 16 * BATCH // 2)

        @block.gpsimd
        def _(gp):
            gp.memset(ident[:, :], 0.0).then_inc(S["ident_on"], 1)
            gp.memset(causal[:, :], 1.0).then_inc(S["mask_on"], 1)
            gp.memset(same_head[:, :], 1.0).then_inc(S["mask_on"], 1)
            gp.memset(ones[:, :], 1.0).then_inc(S["const_on"], 1)
            gp.memset(neg_half[:, :], -0.5).then_inc(S["const_on"], 1)
            gp.wait_ge(S["ident_on"], 1)
            gp.affine_select(out=ident[:, :], in_=ident[:, :], compare_op=ALU.not_equal, fill=1.0,
                             base=0, pattern=[[-1, P]], channel_multiplier=1).then_inc(S["ident_on"], 1)
            gp.wait_ge(S["mask_on"], 2)
            gp.affine_select(out=causal[:, :], in_=causal[:, :], compare_op=ALU.is_ge, fill=0.0,
                             base=0, pattern=[[1, P]], channel_multiplier=-1).then_inc(S["mask_on"], 1)
            heads = same_head[:, :].rearrange("p (h d) -> p h d", d=HD)
            gp.affine_select(out=heads, in_=heads, compare_op=ALU.is_ge, fill=0.0,
                             base=0, pattern=[[-HD, HPH], [0, HD]], channel_multiplier=1)\
                .then_inc(S["mask_on"], 1)
            gp.wait_ge(S["mask_on"], 4)
            gp.affine_select(out=heads, in_=heads, compare_op=ALU.is_ge, fill=0.0,
                             base=HD - 1, pattern=[[HD, HPH], [0, HD]], channel_multiplier=-1)\
                .then_inc(S["mask_on"], 1)
            exact = dict(allow_small_or_imprecise_dtypes=True)
            gp.iota(iota_p[:, :], [[0, 1]], base=0, channel_multiplier=1, **exact).then_inc(S["const_on"], 1)
            gp.iota(iota_128[:, :], [[1, P]], base=0, channel_multiplier=0, **exact).then_inc(S["const_on"], 1)
            gp.iota(iota_list[:, :], [[1, LISTS]], base=0, channel_multiplier=0, **exact)\
                .then_inc(S["const_on"], 1)
            gp.iota(iota_exp[:, :], [[1, EXPERTS]], base=0, channel_multiplier=0, **exact)\
                .then_inc(S["const_on"], 1)
            gp.iota(slot_base[:, :], [[CAP, EXPERTS]], base=-1 - NO_SLOT, channel_multiplier=0, **exact)\
                .then_inc(S["const_on"], 1)
            gp.iota(tile_no[:, :, :], [[1, TILES], [0, 2]], base=0, channel_multiplier=0, **exact)\
                .then_inc(S["const_on"], 1)
            def norm1(b):
                hold(gp, S["mean1"], TILES * (b.n + 1))
                base = 3 * b.n
                gp.tensor_scalar(var1[:, :], mv1[:, :, 1], EPS, None, ALU.add).then_inc(S["rstd1_on"], 1)
                gp.tensor_scalar(negm1[:, :], mv1[:, :, 0], -1.0, None, ALU.mult).then_inc(S["rstd1_on"], 1)
                wait(gp, S["rstd1_on"], base + 2)
                gp.tensor_tensor(rstd1[:, :], var1[:, :], neg_half[:, :], ALU.pow).then_inc(S["rstd1_on"], 1)
                wait(gp, S["rstd1_on"], base + 3)
                hold(gp, S["pe_front"], 11 * (b.n - 1) + 2)
                for t in range(TILES):
                    gp.tensor_scalar(xn[:, t, :], x_sb[b.p][:, t, :], negm1[:, t:t + 1], rstd1[:, t:t + 1],
                                     ALU.add, ALU.mult).then_inc(S["xn_on"], 1)

            def q_times_kcum(b):
                for k in range(KH):
                    wait(gp, S["kcum_on"], KH * b.n + k + 1)
                    gp.tensor_tensor(qk[:, k, :], qT[b.p][:, k, :], kcum[:, k, :], ALU.mult)\
                        .then_inc(S["qk_on"], 1)

            def gate_out(b):
                if isinstance(b.n, int) and b.n == 0:
                    wait(gp, S["bo_on"], 1)
                wait(gp, ga_in[b.p], 16 * (b.h + 1))
                gp.tensor_tensor(bo_g[:, :], bo_all[:, :], ga_all[b.p][:, :], ALU.mult)\
                    .then_inc(S["bog_on"], 1)
                wait(gp, S["bog_on"], b.n + 1)
                wait(gp, S["h2a_on"], TILES * (b.n - 1))
                wait(gp, x1_out[b.p], 16 * b.h)
                gp.tensor_tensor(x1[b.p][:, :, :], x_sb[b.p][:, :, :],
                                 bo_g[:, :].unsqueeze(1).to_broadcast([P, TILES, D]), ALU.add)\
                    .then_inc(S["xb_on"], 1)
                wait(gp, S["wo_mm"], TILES * b.n)
                for k in range(KH):
                    gp.tensor_tensor(wog[:, k, :], wo_sb[:, k, :], ga_all[b.p][:, :], ALU.mult)\
                        .then_inc(S["wog_on"], 1)

            def norm2(b):
                hold(gp, S["mean2"], TILES * (b.n + 1))
                gp.tensor_scalar(var2[:, :], mv2[:, :, 1], EPS, None, ALU.add).then_inc(S["rstd2_on"], 1)
                wait(gp, S["rstd2_on"], 2 * b.n + 1)
                gp.tensor_tensor(rstd2[:, :], var2[:, :], neg_half[:, :], ALU.pow).then_inc(S["rstd2_on"], 1)

            def step(early, front, attend, route):
                if attend:
                    gate_out(attend)
                if route:
                    norm2(route)
                if front:
                    q_times_kcum(front)
                if early:
                    norm1(early)
                    if isinstance(early.n, int) and early.n == 0:
                        gp.memset(q_wide[0][:, :, :, :], 0.0).then_inc(S["zero_q0"], 1)
                        gp.memset(q_wide[1][:, :, :, :], 0.0).then_inc(S["zero_q1"], 1)

            steps(gp, step)

            def gather(e, q):
                wait(gp, S["gT_mm"], KH * (e - 1))
                wait(gp, S["aside_on"], e - 1)
                gp.tensor_copy(list_in[q][:, :], tok_i[:, 0, bass.ds(SLOT_TILES * e, SLOT_TILES)])\
                    .then_inc(S["list_ld"], 1)
                hold(gp, S["list_ld"], e + 1)
                for t in range(SLOT_TILES):
                    gp.indirect_dma_start(
                        out=xg[q][:, t, :], out_offset=None, in_=rows,
                        in_offset=bass.IndirectOffsetOnAxis(ap=list_in[q][:, t:t + 1], axis=0),
                        bounds_check=TOKENS - 1, oob_is_err=False).then_inc(gathered[q], 16)

            def scatter(e, q):
                wait(gp, S["scat"], 16 * SLOT_TILES * e)
                gp.tensor_copy(list_back[q][:, :], tok_i[:, 1, bass.ds(SLOT_TILES * e, SLOT_TILES)])\
                    .then_inc(S["back_ld"], 1)
                hold(gp, S["back_ld"], e + 1)
                for t in range(SLOT_TILES):
                    hold(gp, S["y_on"], SLOT_TILES * e + t + 1)
                    gp.indirect_dma_start(
                        out=out_rows,
                        out_offset=bass.IndirectOffsetOnAxis(ap=list_back[q][:, t:t + 1], axis=0),
                        in_=y_sb[q][:, t, :], in_offset=None,
                        bounds_check=TOKENS - 1, oob_is_err=False, compute_op=ALU.add)\
                        .then_inc(S["scat"], 16)

            wait(gp, S["tok_on"], 4)
            wait(gp, rows_out, 32 * BATCH)
            for p in range(2):
                wait(gp, x1_out[p], 16 * BATCH // 2)
            for e in range(4):
                gather(e, e % 2)
            scatter(0, 0)
            with gp.Fori(1, EXPERTS // 2 - 1) as i:
                gather(2 * i + 2, 0)
                scatter(2 * i - 1, 1)
                gather(2 * i + 3, 1)
                scatter(2 * i, 0)
            for e in range(EXPERTS - 3, EXPERTS):
                scatter(e, e % 2)

        @block.scalar
        def _(act):
            act.wait_ge(S["c_in"], 16)
            act.activation(c_exp[:, :, :], c_sb[:, :, :], ACT.Exp, scale=-1.0).then_inc(S["c_neg"], 1)

            def front_h(b):
                for k in range(KH):
                    wait(act, S["pe_front"], 11 * b.n + k + 1)
                    act.activation(h1T[:, k, :], ring[k][:, :], ACT.Identity,
                                   bias=mod_T[:, 0, k, bass.ds(b.n, 1)],
                                   scale=mod_T[:, 1, k, bass.ds(b.n, 1)]).then_inc(S["h1T_on"], 1)

            def front_exp_q(b):
                for k in range(KH):
                    wait(act, S["q_min"], KH * b.n + k + 1)
                    act.activation(q_exp[:, k, :], q_exp[:, k, :], ACT.Exp).then_inc(S["q_expd"], 1)

            def front_exp_k(b):
                wait(act, den_out, 16 * b.n)
                for k in range(KH):
                    wait(act, S["pe_front"], 11 * b.n + 5 + k)
                    act.activation(k_exp[:, k, :], ring[k][:, :], ACT.Relu, bias=neg_bk[:, k:k + 1],
                                   scale=-1.0).then_inc(S["k_expd"], 1)
                    wait(act, S["k_expd"], 2 * KH * b.n + 2 * k + 1)
                    act.activation(k_exp[:, k, :], k_exp[:, k, :], ACT.Exp, scale=-1.0)\
                        .then_inc(S["k_expd"], 1)

            def front_v(b):
                for r in range(2):
                    wait(act, S["pe_front"], 11 * b.n + 7 + r)
                    for t in range(2):
                        act.activation(v_pad[b.p][:, 2 * r + t, :, 0:4:3, :],
                                       ring[r][:, t * D:(t + 1) * D]
                                       .rearrange("p (a b c) -> p a b c", b=2, c=HD), ACT.Copy)\
                            .then_inc(S["v_on"], 1)

            def front_kt(b):
                for r in range(2):
                    wait(act, S["pe_front"], 11 * b.n + 9 + r)
                    n = 2 if r == 0 else TILES - 3
                    act.activation(k_tok[b.p][:, 2 * r:2 * r + n, :],
                                   ring[r][:, 0:n * D].rearrange("p (t d) -> p t d", d=D), ACT.Copy)\
                        .then_inc(S["k_tok_on"], 1)

            def front_den(b):
                wait(act, S["pe_front"], 11 * b.n + 11)
                wait(act, S["k_on"], KH * (b.n + 1))
                act.activation(den_sb, ring[0][0:HEADS, :], ACT.Copy).then_inc(S["den_on"], 1)

            def route_h(b):
                for k in range(KH):
                    wait(act, S["pe_route"], 5 * b.n + k + 1)
                    act.activation(h2T[:, k, :], rt_bank[:, :], ACT.Copy).then_inc(S["h2T_on"], 1)

            def route_e(b):
                wait(act, S["gap_on"], b.n + 1)
                act.activation(e2[:, :], gap[:, :], ACT.Exp).then_inc(S["e2_on"], 1)

            def step(early, front, attend, route):
                if front:
                    if isinstance(front.n, int) and front.n == 0:
                        wait(act, S["modT_on"], 1)
                        wait(act, S["bias_on"], 2)
                        wait(act, S["zero_v"], 2)
                    front_h(front)
                    front_exp_q(front)
                if route:
                    route_h(route)
                if front:
                    front_exp_k(front)
                if route:
                    route_e(route)
                if front:
                    front_v(front)
                    front_kt(front)
                    front_den(front)

            steps(act, step)

            def turn_rows(e, q):
                for k in range(KH):
                    wait(act, S["gT_mm"], KH * e + k + 1)
                    act.activation(xgT[q][:, k, :], bank[k][:, :], ACT.Copy).then_inc(S["xgT_on"], 1)
                wait(act, S["y_on"], SLOT_TILES * (e - 1))
                act.activation(aside[q], xg[q][:, :, ROW_W:ROW], ACT.Copy).then_inc(S["aside_on"], 1)

            def relu(e, q):
                for i in range(0, IB, 2):
                    wait(act, S["m1_mm"], IB * e + i + 1)
                    act.activation(inner[q][:, i, :], bank[2 + i][:, :], ACT.Relu).then_inc(S["relu_a"], 1)

            turn_rows(0, 0)
            relu(0, 0)
            turn_rows(1, 1)
            relu(1, 1)
            turn_rows(2, 0)
            with act.Fori(1, EXPERTS // 2 - 1) as i:
                relu(2 * i, 0)
                turn_rows(2 * i + 1, 1)
                relu(2 * i + 1, 1)
                turn_rows(2 * i + 2, 0)
            relu(EXPERTS - 2, 0)
            turn_rows(EXPERTS - 1, 1)
            relu(EXPERTS - 1, 1)

        @block.tensor
        def _(pe):
            mm = nc.tensor.matmul
            pe.wait_ge(S["silu_on"], 3)

            def modulate(j):
                pe.wait_ge(wmod_in[j], 16)
                for k in range(KH):
                    last = mm(bank[4 + j][0:BATCH, :], silu[:, k, :], wmod_sb[j][:, k, :],
                              start=(k == 0), stop=(k == KH - 1))
                last.then_inc(S["mod_mm"], 1)
            modulate(0)
            modulate(1)
            pe.wait_ge(S["ident_on"], 2)
            pe.wait_ge(S["mod_ev"], 2)
            for j in range(2):
                for k in range(KH):
                    last = nc.tensor.transpose(bank[3][:, (j * KH + k) * BATCH:(j * KH + k + 1) * BATCH],
                                               mod_sb[:, j, k * P:(k + 1) * P], ident[0:BATCH, 0:BATCH])
            last.then_inc(S["mod_t"], 1)
            modulate(2)
            pe.wait_ge(S["bvw_on"], KH)
            pe.wait_ge(S["w_in"], 16 * 7)
            pe.wait_ge(S["const_on"], 2)
            for k in range(KH):
                mm(bank[2][:, 0:D], bv_wide[:, k, :], wo_sb[:, k, :], start=(k == 0), stop=False)
            mm(bank[2][:, 0:D], ones[0:1, 0:P], bo_row[:, :], start=False, stop=True).then_inc(S["bo_mm"], 1)
            pe.wait_ge(S["mask_on"], 5)
            pe.wait_ge(S["head_on"], 3)

            def front_h(b):
                wait(pe, S["xn_on"], TILES * (b.n + 1))
                for k in range(KH):
                    if k == 0:
                        wait(pe, S["den_on"], b.n)
                    else:
                        wait(pe, S["k_tok_on"], 2 * b.n)
                    for t in range(TILES):
                        last = nc.tensor.transpose(ring[k][:, tok(t)], xn[:, t, k * P:(k + 1) * P],
                                                   ident[:, :])
                    last.then_inc(S["pe_front"], 1)

            def project(w, b, done, count):
                for m in range(KH):
                    wait(pe, done, count + m)
                    for k in range(KH):
                        last = mm(ring[m][:, :], w[:, k, m * P:(m + 1) * P], h1T[:, k, :],
                                  start=(k == 0), stop=(k == KH - 1))
                    last.then_inc(S["pe_front"], 1)

            def front_q(b):
                wait(pe, S["h1T_on"], KH * (b.n + 1))
                project(wq_sb, b, S["h1T_on"], KH * b.n + 1)

            def front_k(b):
                project(wk_sb, b, S["q_on"], KH * b.n + 1)

            def front_v(b):
                for r in range(2):
                    wait(pe, S["k_on"], KH * b.n + r + 1)
                    for t in range(2):
                        for k in range(KH):
                            last = mm(ring[r][:, t * D:(t + 1) * D], h1T[:, k, tok(2 * r + t)],
                                      wv_sb[:, k, :], start=(k == 0), stop=(k == KH - 1))
                    last.then_inc(S["pe_front"], 1)

            def front_kt(b):
                wait(pe, S["k_on"], KH * (b.n + 1))
                for r in range(2):
                    wait(pe, S["v_on"], 4 * b.n + 2 * r + 2)
                    for t in range(2 if r == 0 else TILES - 3):
                        for k in range(KH):
                            last = nc.tensor.transpose(ring[r][:, t * D + k * P:t * D + (k + 1) * P],
                                                       kT[b.p][:, k, tok(2 * r + t)], ident[:, :])
                    last.then_inc(S["pe_front"], 1)

            def front_den(b):
                wait(pe, S["k_tok_on"], 2 * b.n + 1)
                wait(pe, S["qk_on"], KH * (b.n + 1))
                for k in range(KH):
                    last = mm(ring[0][0:HEADS, :], head_sum[:, k, :], qk[:, k, :], start=(k == 0),
                              stop=(k == KH - 1))
                last.then_inc(S["pe_front"], 1)

            def scores(b, t):
                for g in range(QUADS):
                    k, quad = divmod(g, QUADS // KH)
                    use = TILES * QUADS * b.n + QUADS * t + g
                    if t == 0 and quad == 0:
                        wait(pe, q_wide_in[b.p][k], 16 * HPH * (b.h + 1))
                    wait(pe, S["masked"], use - 1)
                    mm(sc_bank[g % 2][:, :].rearrange("p (h i) -> p h i", h=4), kT[b.p][:, k, tok(t)],
                       q_wide[b.p][:, k, 4 * quad:4 * quad + 4, tok(t)], start=True, stop=True)\
                        .then_inc(S["sc_on"], 1)

            def numerator(b, t):
                wait(pe, S["masked"], QUADS * (TILES * b.n + t + 1))
                wait(pe, S["oT_on"], TILES * b.n + t)
                if t == 0:
                    wait(pe, S["v_on"], 4 * (b.n + 1))
                else:
                    wait(pe, S["state_on"], (TILES - 1) * b.n + t)
                    for k in range(KH):
                        mm(oT_bank[:, k * P:(k + 1) * P], state[(t - 1) % 2][:, k, :], qT[b.p][:, k, tok(t)],
                           start=True, stop=False, skip_group_check=True)
                        heads_of(b, t, k)
                    return
                for k in range(KH):
                    heads_of(b, t, k)

            def heads_of(b, t, k):
                for h in range(HPH):
                    head = k * HPH + h
                    at = 32 * (h // 2)
                    pair = v_pad[b.p][:, t, head // 2, :, :].rearrange("p a b -> p (a b)")
                    last = mm(oT_bank[at:at + 32, k * P:(k + 1) * P], pair[:, 32 * (h % 2):32 * (h % 2) + 32],
                              sT[t % 2][:, head, :], start=(t == 0 and h % 2 == 0), stop=(h % 2 == 1),
                              skip_group_check=True)
                if k == KH - 1:
                    last.then_inc(S["oT_mm"], 1)

            def update_state(b, t):
                if t == 0:
                    wait(pe, S["k_tok_on"], 2 * (b.n + 1))
                    wait(pe, S["v_on"], 4 * (b.n + 1))
                wait(pe, S["state_on"], (TILES - 1) * b.n + t)
                for k in range(KH):
                    last = mm(kv_bank[:, k * P:(k + 1) * P].rearrange("p (a b c) -> p a b c", b=2, c=HD),
                              k_tok[b.p][:, t, k * P:(k + 1) * P],
                              v_pad[b.p][:, t, k * HPH // 2:(k + 1) * HPH // 2, 0:4:3, :],
                              start=(t == 0 and k == 0), stop=(t == TILES - 2), skip_group_check=True)
                last.then_inc(S["kv_mm"], 1)

            def out_project(b, t):
                wait(pe, S["oT_on"], TILES * b.n + t + 1)
                wait(pe, S["wog_on"], KH * (b.n + 1))
                wait(pe, S["x1_on"], TILES * b.n + t)
                for k in range(KH):
                    last = mm(wo_bank[:, 0:D], oT[t % 2][:, k, :], wog[:, k, :], start=(k == 0),
                              stop=(k == KH - 1))
                last.then_inc(S["wo_mm"], 1)

            def route_h(b, k):
                wait(pe, S["h2_on"], TILES * (b.n + 1))
                if k == 0:
                    wait(pe, S["lists_on"], b.n)
                else:
                    wait(pe, S["h2T_on"], KH * b.n + k)
                for t in range(TILES):
                    last = nc.tensor.transpose(rt_bank[:, tok(t)], h2[:, t, k * P:(k + 1) * P],
                                               ident[:, :])
                last.then_inc(S["pe_route"], 1)

            def route_logits(b):
                wait(pe, S["h2T_on"], KH * (b.n + 1))
                for t in range(TILES):
                    for k in range(KH):
                        last = mm(rt_bank[:, t * EXPERTS:(t + 1) * EXPERTS], h2T[:, k, tok(t)],
                                  emb_sb[:, k, :], start=(k == 0), stop=(k == KH - 1))
                last.then_inc(S["pe_route"], 1)

            def route_counts(b):
                wait(pe, S["oh_on"], b.n + 1)
                wait(pe, S["logits_on"], b.n + 1)
                n = TILES * EXPERTS
                mm(rt_bank[:, 0:n], causal_bf[:, :], both_bf[:, :, :].rearrange("p t e -> p (t e)"),
                   start=True, stop=False)
                mm(rt_bank[:, 0:n], ones_bf[:, :], counts_bf[:, :, :].rearrange("p t e -> p (t e)"),
                   start=False, stop=True).then_inc(S["pe_route"], 1)

            def route_lists(b):
                wait(pe, S["slots_on"], b.n + 1)
                for c in range(2 * TILES):
                    last = mm(rt_bank[:, 0:3 * LISTS], in_slot[:, c, :],
                              in_list[:, c, :, :].rearrange("p a l -> p (a l)"), start=(c == 0),
                              stop=(c == 2 * TILES - 1))
                last.then_inc(S["pe_route"], 1)

            def step(early, front, attend, route):
                if attend:
                    scores(attend, 0)
                if route:
                    out_project(route, 3)
                if front:
                    front_h(front)
                if attend:
                    update_state(attend, 0)
                    scores(attend, 1)
                if front:
                    front_q(front)
                if route:
                    route_h(route, 0)
                if attend:
                    numerator(attend, 0)
                if route:
                    route_h(route, 1)
                if front:
                    front_k(front)
                if attend:
                    out_project(attend, 0)
                    update_state(attend, 1)
                if route:
                    route_logits(route)
                if attend:
                    scores(attend, 2)
                    numerator(attend, 1)
                if front:
                    front_v(front)
                if attend:
                    out_project(attend, 1)
                if route:
                    route_counts(route)
                if attend:
                    update_state(attend, 2)
                    scores(attend, 3)
                if front:
                    front_kt(front)
                if attend:
                    numerator(attend, 2)
                if front:
                    front_den(front)
                if attend:
                    out_project(attend, 2)
                    numerator(attend, 3)
                if route:
                    route_lists(route)

            steps(pe, step)

            def turn_rows(e, q):
                wait(pe, gathered[q], (e // 2 + 1) * 16 * SLOT_TILES if isinstance(e, int)
                     else (e + 2 - q) * 8 * SLOT_TILES)
                for k in range(KH):
                    wait(pe, S["xgT_on"], KH * (e - 1) + k + 1)
                    for t in range(SLOT_TILES):
                        last = nc.tensor.transpose(bank[k][:, tok(t)], xg[q][:, t, k * P:(k + 1) * P],
                                                   ident[:, :])
                    last.then_inc(S["gT_mm"], 1)

            def up(e, q):
                wait(pe, S["xgT_on"], KH * (e + 1))
                wait(pe, exp_w_in[q], 32 * (e // 2 + 1) if isinstance(e, int) else (e + 2 - q) * 16)
                for i in range(IB):
                    wait(pe, S["relu_v" if i % 2 else "relu_a"], IB // 2 * (e - 1) + i // 2 + 1)
                    for k in range(KH):
                        last = mm(bank[2 + i][:, :], w1_sb[q][:, k, i * P:(i + 1) * P], xgT[q][:, k, :],
                                  start=(k == 0), stop=(k == KH - 1))
                    last.then_inc(S["m1_mm"], 1)

            def down(e, q):
                wait(pe, S["relu_a"], IB // 2 * (e + 1))
                wait(pe, S["relu_v"], IB // 2 * (e + 1))
                for t in range(SLOT_TILES):
                    wait(pe, S["y_on"], SLOT_TILES * e + t - 1)
                    for i in range(IB):
                        last = mm(bank[6 + t % 2][:, 0:D], inner[q][:, i, tok(t)], w2_sb[q][:, i, :],
                                  start=(i == 0), stop=(i == IB - 1))
                    last.then_inc(S["m2_mm"], 1)

            wait(pe, S["lists_on"], BATCH)
            turn_rows(0, 0)
            up(0, 0)
            turn_rows(1, 1)
            down(0, 0)
            with pe.Fori(1, EXPERTS // 2) as i:
                up(2 * i - 1, 1)
                turn_rows(2 * i, 0)
                down(2 * i - 1, 1)
                up(2 * i, 0)
                turn_rows(2 * i + 1, 1)
                down(2 * i, 0)
            up(EXPERTS - 1, 1)
            down(EXPERTS - 1, 1)

        @block.vector
        def _(dve):
            v = nc.vector
            v.memset(v_pad[0][:, :, :, :, :], 0.0).then_inc(S["zero_v"], 1)
            dve.wait_ge(S["c_neg"], 1)
            v.tensor_scalar(c_exp[:, :, :], c_exp[:, :, :], 1.0, None, ALU.add).then_inc(S["silu_on"], 1)
            dve.wait_ge(S["silu_on"], 1)
            v.reciprocal(c_exp[:, :, :], c_exp[:, :, :]).then_inc(S["silu_on"], 1)
            dve.wait_ge(S["silu_on"], 2)
            v.tensor_tensor(silu[:, :, :], c_sb[:, :, :], c_exp[:, :, :], ALU.mult).then_inc(S["silu_on"], 1)
            v.memset(v_pad[1][:, :, :, :, :], 0.0).then_inc(S["zero_v"], 1)
            v.memset(ones_bf[:, :], 1.0)
            v.memset(counts[:, :, :], 0.0)
            v.memset(lists[:, :, :], 0.0)
            v.memset(head_sum[:, :, :], 0.0).then_inc(S["head_on"], 1)
            dve.wait_ge(S["mask_on"], 5)
            dve.wait_ge(S["const_on"], 8)
            v.tensor_copy(causal_bf[:, :], causal[:, :])
            dve.wait_ge(S["head_on"], 1)
            for k in range(KH):
                v.tensor_copy(head_sum[:, k, k * HPH:(k + 1) * HPH], same_head[:, 0:P:HD])\
                    .then_inc(S["head_on"], 1)

            def setup():
                for j in range(3):
                    dve.wait_ge(S["mod_mm"], j + 1)
                    v.tensor_copy(mod_sb[:, 2 * j:2 * j + 2, :],
                                  bank[4 + j][0:BATCH, :].rearrange("b (m d) -> b m d", m=2))\
                        .then_inc(S["mod_ev"], 1)
                    if j == 0:
                        dve.wait_ge(S["mod_ev"], 1)
                        v.tensor_scalar(mod_sb[:, CA, :], mod_sb[:, CA, :], 1.0, None, ALU.add)\
                            .then_inc(S["mod_ev"], 1)
                        dve.wait_ge(S["w_in"], 16 * 7)
                        v.tensor_scalar(bias_p1[:, :, :], bias_in[:, 0:2, :], 1.0, None, ALU.add)\
                            .then_inc(S["bias_on"], 1)
                        v.tensor_scalar(neg_bk[:, :], bias_in[:, 1, :], -1.0, None, ALU.mult)\
                            .then_inc(S["bias_on"], 1)
                        for k in range(KH):
                            v.tensor_scalar(bv_wide[:, k, :], ones[:, 0:P], bias_in[:, 2, k:k + 1], None,
                                            ALU.mult).then_inc(S["bvw_on"], 1)
                        dve.wait_ge(S["mod_t"], 1)
                        v.tensor_copy(mod_T[:, :, :, :],
                                      bank[3][:, 0:2 * KH * BATCH]
                                      .rearrange("p (j k b) -> p j k b", j=2, k=KH)).then_inc(S["modT_on"], 1)
                dve.wait_ge(S["mod_ev"], 4)
                v.tensor_scalar(mod_sb[:, CB, :], mod_sb[:, CB, :], 1.0, None, ALU.add)\
                    .then_inc(S["gate_on"], 1)
                gates = mod_sb[:, GA:MODS:GB - GA, :]
                v.scalar_tensor_tensor(out=mod_abs[:, :, :], in0=gates, scalar=-1.0, in1=gates,
                                       op0=ALU.mult, op1=ALU.max).then_inc(S["gate_on"], 1)
                v.tensor_scalar(mod_sign[:, :, :], gates, 0.0, 2.0, ALU.is_ge, ALU.mult)\
                    .then_inc(S["gate_on"], 1)
                dve.wait_ge(S["gate_on"], 3)
                v.tensor_scalar(mod_abs[:, :, :], mod_abs[:, :, :], 0.25, None, ALU.max)\
                    .then_inc(S["bias_on"], 1)
                dve.wait_ge(S["bias_on"], 3)
                v.scalar_tensor_tensor(out=gates, in0=mod_sign[:, :, :], scalar=-1.0, in1=mod_abs[:, :, :],
                                       op0=ALU.add, op1=ALU.mult).then_inc(S["gate_on"], 1)
                dve.wait_ge(S["bo_mm"], 1)
                v.tensor_copy(bo_all[:, :], bank[2][:, 0:D]).then_inc(S["bo_on"], 1)

            def early_stats(b):
                wait(dve, x_in[b.p], 16 * (b.h + 1))
                for t in range(TILES):
                    v.bn_stats(stat1[:, t, :], x_sb[b.p][:, t, :]).then_inc(S["stats1"], 1)
                hold(dve, S["stats1"], TILES * (b.n + 1))
                for t in range(TILES):
                    v.bn_aggr(mv1[:, t, :], stat1[:, t, :]).then_inc(S["mean1"], 1)

            def front_q(b):
                for k in range(KH):
                    wait(dve, S["pe_front"], 11 * b.n + 3 + k)
                    v.tensor_scalar(q_exp[:, k, :], ring[k][:, :], bias_in[:, 0, k:k + 1], 0.0,
                                    ALU.add, ALU.min).then_inc(S["q_min"], 1)
                for k in range(KH):
                    wait(dve, S["q_expd"], KH * b.n + k + 1)
                    v.scalar_tensor_tensor(out=qT[b.p][:, k, :], in0=ring[k][:, :], scalar=bias_p1[:, 0, k:k + 1],
                                           in1=q_exp[:, k, :], op0=ALU.add, op1=ALU.max)\
                        .then_inc(S["q_on"], 1)

            def front_k(b):
                for k in range(KH):
                    wait(dve, S["k_expd"], 2 * KH * b.n + 2 * k + 2)
                    v.scalar_tensor_tensor(out=kT[b.p][:, k, :], in0=ring[k][:, :],
                                           scalar=bias_p1[:, 1, k:k + 1], in1=k_exp[:, k, :],
                                           op0=ALU.add, op1=ALU.max).then_inc(S["k_on"], 1)
                for k in range(KH):
                    wait(dve, S["k_on"], KH * b.n + k + 1)
                    v.tensor_tensor_scan(kcum[:, k, :], ones[:, :], kT[b.p][:, k, :], 0.0,
                                         ALU.mult, ALU.add).then_inc(S["kcum_on"], 1)

            def invert_den(b):
                wait(dve, den_in, 16 * (b.n + 1))
                wait(dve, rden_out, 16 * b.n)
                v.reciprocal(rden_flat[:, :], den_flat[:, :]).then_inc(S["rden_on"], 1)

            def normalise(b, t):
                if t == 0:
                    wait(dve, rden_in[b.p], 16 * HPH * (b.h + 1))
                wait(dve, S["oT_mm"], TILES * b.n + t + 1)
                wait(dve, S["wo_mm"], TILES * b.n + t - 1)
                v.tensor_tensor(oT[t % 2][:, :, :], oT_bank[:, 0:KH * P].rearrange("p (k i) -> p k i", k=KH),
                                rden[b.p][:, :, tok(t)], ALU.mult).then_inc(S["oT_on"], 1)

            def mask(b, t):
                for g in range(QUADS):
                    use = TILES * QUADS * b.n + QUADS * t + g
                    if g == 0:
                        wait(dve, S["oT_mm"], TILES * b.n + t - 1)
                    wait(dve, S["sc_on"], use + 1)
                    v.tensor_tensor(sT[t % 2][:, 4 * g:4 * g + 4, :],
                                    sc_bank[g % 2][:, :].rearrange("p (h i) -> p h i", h=4),
                                    causal[:, :].unsqueeze(1).to_broadcast([P, 4, P]), ALU.mult)\
                        .then_inc(S["masked"], 1)

            def keep_state(b, t):
                wait(dve, S["kv_mm"], (TILES - 1) * b.n + t + 1)
                wait(dve, S["oT_mm"], TILES * b.n + t)
                v.tensor_tensor(state[t % 2][:, :, :],
                                kv_bank[:, 0:KH * P].rearrange("p (k e) -> p k e", k=KH),
                                same_head[:, :].unsqueeze(1).to_broadcast([P, KH, P]), ALU.mult)\
                    .then_inc(S["state_on"], 1)

            def residual(b, t):
                if t == 0:
                    wait(dve, S["xb_on"], b.n + 1)
                wait(dve, S["wo_mm"], TILES * b.n + t + 1)
                v.tensor_tensor(x1[b.p][:, t, :], wo_bank[:, 0:D], x1[b.p][:, t, :], ALU.add)\
                    .then_inc(S["x1_on"], 1)
                wait(dve, S["x1_on"], TILES * b.n + t + 1)
                v.bn_stats(stat2[:, t, :], x1[b.p][:, t, :]).then_inc(S["stats2"], 1)

            def mean2(b):
                hold(dve, S["stats2"], TILES * (b.n + 1))
                for t in range(TILES):
                    v.bn_aggr(mv2[:, t, :], stat2[:, t, :]).then_inc(S["mean2"], 1)

            def route_h(b):
                wait(dve, S["mean2"], TILES * (b.n + 1))
                wait(dve, mod_in[b.p], 16 * (b.h + 1))
                wait(dve, rows_out, 32 * b.n)
                for t in range(TILES):
                    v.scalar_tensor_tensor(out=h2[:, t, 0:D], in0=x1[b.p][:, t, :], scalar=mv2[:, t, 0:1],
                                           in1=mod_all[b.p][:, 1, :], op0=ALU.subtract, op1=ALU.mult)\
                        .then_inc(S["h2a_on"], 1)
                wait(dve, S["rstd2_on"], 2 * (b.n + 1))
                for t in range(TILES):
                    wait(dve, S["h2a_on"], TILES * b.n + t + 1)
                    v.scalar_tensor_tensor(out=h2[:, t, 0:D], in0=h2[:, t, 0:D], scalar=rstd2[:, t:t + 1],
                                           in1=mod_all[b.p][:, 0, :], op0=ALU.mult, op1=ALU.add)\
                        .then_inc(S["h2_on"], 1)

            def chain(b):
                done = [0]

                def mark(ins, sync=True):
                    ins.then_inc(S["small"], 1)
                    done[0] += 1
                    if sync:
                        wait(dve, S["small"], SMALL * b.n + done[0])
                return done, mark

            te = [P, TILES, EXPERTS]

            def route_top(b):
                wait(dve, S["pe_route"], 5 * b.n + 3)
                v.tensor_copy(logits[:, :, :],
                              rt_bank[:, 0:TILES * EXPERTS].rearrange("p (t e) -> p t e", t=TILES))\
                    .then_inc(S["logits_on"], 1)
                hold(dve, S["logits_on"], b.n + 1)
                for t in range(TILES):
                    v.max(top[:, t, :], logits[:, t, :]).then_inc(S["top_on"], 1)
                hold(dve, S["top_on"], TILES * (b.n + 1))
                for t in range(TILES):
                    v.max_index(top_i[:, t, :], top[:, t, :], logits[:, t, :]).then_inc(S["topi_on"], 1)
                v.tensor_tensor(gap[:, :], top[:, :, 1], top[:, :, 0], ALU.subtract).then_inc(S["gap_on"], 1)
                wait(dve, S["topi_on"], TILES * (b.n + 1))

            def route_choose(b, mark):
                mark(v.tensor_copy(top_f[:, :, :], top_i[:, :, 0:2]))
                for j in range(2):
                    mark(v.tensor_tensor(one_hot[:, j, :, :], iota_exp[:, :].unsqueeze(1).to_broadcast(te),
                                         top_f[:, :, j:j + 1].to_broadcast(te), ALU.is_equal), sync=False)
                wait(dve, S["e2_on"], b.n + 1)
                mark(v.tensor_scalar(wsum[:, :], e2[:, :], 1.0, None, ALU.add))
                mark(v.reciprocal(w12[:, 0, :], wsum[:, :]))
                mark(v.tensor_tensor(w12[:, 1, :], e2[:, :], w12[:, 0, :], ALU.mult))
                mark(v.tensor_scalar(alive[:, :], w12[:, 1, :], 0.0, None, ALU.is_gt))
                mark(v.tensor_tensor(one_hot[:, 1, :, :], one_hot[:, 1, :, :],
                                     alive[:, :].unsqueeze(2).to_broadcast(te), ALU.mult))
                mark(v.tensor_tensor(both_bf[:, :, :], one_hot[:, 0, :, :], one_hot[:, 1, :, :], ALU.add))
                for t in range(TILES):
                    mark(v.tensor_tensor(counts[:, t + 1, :], counts[:, t, :], both_bf[:, t, :], ALU.add))
                v.tensor_copy(counts_bf[:, :, :], counts[:, 0:TILES, :]).then_inc(S["oh_on"], 1)
                for j in range(2):
                    mark(v.tensor_tensor(weighted[:, j, :, :], one_hot[:, j, :, :],
                                         w12[:, j, :].unsqueeze(2).to_broadcast(te), ALU.mult))
                v.tensor_tensor(h2[:, :, D:D + EXPERTS], weighted[:, 0, :, :], weighted[:, 1, :, :], ALU.add)\
                    .then_inc(S["w8_on"], 1)
                wait(dve, S["oh_on"], b.n + 1)
                mark(v.tensor_copy(counts[:, 0, :], counts[:, TILES, :]))

            def route_slots(b, mark):
                wait(dve, S["pe_route"], 5 * b.n + 4)
                count = rt_bank[:, 0:TILES * EXPERTS].rearrange("p (t e) -> p t e", t=TILES)
                mark(v.tensor_scalar(fits[:, :, :], count, float(CAP), None, ALU.is_le), sync=False)
                mark(v.tensor_tensor(slot[:, :, :], count, slot_base[:, :].unsqueeze(1).to_broadcast(te),
                                     ALU.add))
                mark(v.tensor_tensor(slot[:, :, :], slot[:, :, :], fits[:, :, :], ALU.mult))
                for j in range(2):
                    mark(v.tensor_tensor(chosen[:, j, :, :], one_hot[:, j, :, :], slot[:, :, :], ALU.mult))
                    mark(v.tensor_reduce(slot_f[:, :, j], chosen[:, j, :, :], AX.X, ALU.add))
                mark(v.tensor_scalar(slot_i[:, :, :], slot_f[:, :, :], float(NO_SLOT), None, ALU.add))

            def route_places(b, done, mark):
                mark(v.tensor_scalar(part_i[:, 0, :, :], slot_i[:, :, :], P - 1, None, ALU.bitwise_and),
                     sync=False)
                mark(v.tensor_scalar(part_i[:, 1, :, :], slot_i[:, :, :], 7, None, ALU.arith_shift_right))
                mark(v.tensor_copy(part_f[:, :, :, :], part_i[:, :, :, :]))
                shape = [P, 2 * TILES, LISTS]
                list_no = part_f[:, 1, :, :].rearrange("p t j -> p (t j)").unsqueeze(2).to_broadcast(shape)
                mark(v.tensor_tensor(in_list[:, :, 2, :], iota_list[:, :].unsqueeze(1).to_broadcast(shape),
                                     list_no, ALU.is_equal))
                mark(v.tensor_scalar(in_list[:, :, 1, :], in_list[:, :, 2, :], iota_p[:, 0:1], None, ALU.mult),
                     sync=False)
                mark(v.tensor_tensor(in_list[:, :, 0, :], in_list[:, :, 2, :],
                                     tile_no[:, :, :].rearrange("p t j -> p (t j)").unsqueeze(2)
                                     .to_broadcast(shape), ALU.mult))
                mark(v.tensor_scalar(tile_no[:, :, :], tile_no[:, :, :], float(TILES), None, ALU.add),
                     sync=False)
                for c in range(2 * TILES):
                    ins = v.tensor_scalar(in_slot[:, c, :], iota_128[:, :],
                                          part_f[:, 0, c // 2, c % 2:c % 2 + 1], None, ALU.is_equal)
                ins.then_inc(S["slots_on"], 1)
                assert done[0] == SMALL, done

            def route_lists(b):
                wait(dve, S["pe_route"], 5 * (b.n + 1))
                v.tensor_tensor(lists[:, :, :], rt_bank[:, 0:3 * LISTS].rearrange("p (a l) -> p a l", a=3),
                                lists[:, :, :], ALU.add).then_inc(S["lists_on"], 1)

            def step(early, front, attend, route):
                if attend:
                    mask(attend, 0)
                    invert_den(attend)
                if route:
                    residual(route, 3)
                    mean2(route)
                if attend:
                    keep_state(attend, 0)
                    mask(attend, 1)
                if route:
                    route_h(route)
                if front:
                    if isinstance(front.n, int) and front.n == 0:
                        setup()
                    front_q(front)
                if attend:
                    normalise(attend, 0)
                if front:
                    front_k(front)
                if attend:
                    residual(attend, 0)
                    keep_state(attend, 1)
                    mask(attend, 2)
                if route:
                    route_top(route)
                if attend:
                    normalise(attend, 1)
                if route:
                    done, mark = chain(route)
                    route_choose(route, mark)
                if attend:
                    residual(attend, 1)
                    keep_state(attend, 2)
                    mask(attend, 3)
                if route:
                    route_slots(route, mark)
                if attend:
                    normalise(attend, 2)
                if route:
                    route_places(route, done, mark)
                if attend:
                    residual(attend, 2)
                    normalise(attend, 3)
                if early:
                    early_stats(early)
                if route:
                    route_lists(route)

            steps(dve, step)

            dve.wait_ge(S["lists_on"], BATCH)
            v.scalar_tensor_tensor(out=tok_f[:, 0, :], in0=lists[:, 0, :], scalar=float(P), in1=lists[:, 1, :],
                                   op0=ALU.mult, op1=ALU.add).then_inc(S["tok_on"], 1)
            v.tensor_scalar(tok_f[:, 1, :], lists[:, 2, :], -float(TOKENS), float(TOKENS), ALU.mult, ALU.add)\
                .then_inc(S["tok_on"], 1)
            dve.wait_ge(S["tok_on"], 2)
            v.tensor_copy(tok_i[:, 0, :], tok_f[:, 0, :]).then_inc(S["tok_on"], 1)
            v.tensor_tensor(tok_i[:, 1, :], tok_f[:, 1, :], tok_f[:, 0, :], ALU.add).then_inc(S["tok_on"], 1)

            def relu(e, q):
                for i in range(1, IB, 2):
                    wait(dve, S["m1_mm"], IB * e + i + 1)
                    v.tensor_scalar(inner[q][:, i, :], bank[2 + i][:, :], 0.0, None, ALU.max)\
                        .then_inc(S["relu_v"], 1)

            def weigh(e, q):
                wait(dve, S["aside_on"], e + 1)
                v.tensor_copy(w_now[q][:, :].unsqueeze(2), aside[q][:, :, bass.ds(e, 1)])\
                    .then_inc(S["w_ld"], 1)
                wait(dve, S["w_ld"], e + 1)
                for t in range(SLOT_TILES):
                    if t == 0:
                        wait(dve, S["scat"], 16 * SLOT_TILES * (e - 1))
                    wait(dve, S["m2_mm"], SLOT_TILES * e + t + 1)
                    v.scalar_tensor_tensor(out=y_sb[q][:, t, :], in0=bank[6 + t % 2][:, 0:D],
                                           scalar=w_now[q][:, t:t + 1], in1=aside[q][:, t, EXPERTS:],
                                           op0=ALU.mult, op1=ALU.mult).then_inc(S["y_on"], 1)

            for p in range(2):
                dve.wait_ge(x1_out[p], 16 * BATCH // 2)
            for e in range(2):
                relu(e, e)
                weigh(e, e)
            with dve.Fori(1, EXPERTS // 2) as i:
                for q in range(2):
                    relu(2 * i + q, q)
                    weigh(2 * i + q, q)


def kernel(L0_attn_x, L0_attn_Wq, L0_attn_bq, L0_attn_Wk, L0_attn_bk, L0_attn_Wv, L0_attn_bv, L0_attn_Wo,
           L0_attn_bo, L0_ffn_expert_embeddings, L0_ffn_first_linear, L0_ffn_second_linear, L0_c, L0_wmod):
    import numpy as np
    import concourse.bacc as bacc
    from concourse.bass_utils import run_bass_kernel_spmd

    arrays = {
        "x": L0_attn_x,
        "wqT": L0_attn_Wq.T, "wkT": L0_attn_Wk.T, "wvT": L0_attn_Wv.T, "woT": L0_attn_Wo.T,
        "biases": np.stack([L0_attn_bq, L0_attn_bk, L0_attn_bv]).reshape(3, KH, P).transpose(2, 0, 1),
        "bo": L0_attn_bo,
        "embT": L0_ffn_expert_embeddings.T,
        "w1T": L0_ffn_first_linear.transpose(0, 2, 1),
        "w2T": L0_ffn_second_linear.transpose(0, 2, 1),
        "cT": L0_c.T, "wmod": L0_wmod,
    }
    nc = bacc.Bacc("TRN2", target_bir_lowering=False, num_devices=1)
    given, args = {}, []
    for name, a in arrays.items():
        given[name] = np.ascontiguousarray(a)
        args.append(nc.dram_tensor(name, given[name].shape, mybir.dt.from_np(given[name].dtype),
                                   kind="ExternalInput").ap())
    args.append(nc.dram_tensor("out", (BATCH, SEQ, D), F32, kind="ExternalOutput").ap())
    adaln_kernel(nc, *args)
    return run_bass_kernel_spmd(nc, [given], core_ids=[0]).results[0]["out"]
```

```python
from collections import namedtuple
from contextlib import ExitStack

import concourse.bass as bass
from concourse import mybir

F32 = mybir.dt.float32
F32R = mybir.dt.float32r
BF16 = mybir.dt.bfloat16
I32 = mybir.dt.int32
U32 = mybir.dt.uint32
ALU = mybir.AluOpType
ACT = mybir.ActivationFunctionType
AX = mybir.AxisListType

P = 128
BATCH, SEQ, D = 8, 512, 256
HEADS, HD = 16, 16
KH = D // P
TILES = SEQ // P
HPH = P // HD
PAIRS = HEADS // 2
PARTS = 3
STACK = 2 * PARTS * HD
QUADS = HEADS // 4
TOKENS = BATCH * SEQ
EXPERTS, INTER = 8, 512
CAP = -(-TOKENS // EXPERTS)
SLOT_TILES = CAP // P
LISTS = EXPERTS * SLOT_TILES
IB = INTER // P
EPS = 1e-5
NO_SLOT = 2 * EXPERTS * CAP - 1
ROW_W, ROW_G = D, D + EXPERTS
ROW = 2 * D + EXPERTS
MODS = 6
SA, CA, GA, SB, CB, GB = range(MODS)

Batch = namedtuple("Batch", "n h p")


def batch(h, p):
    return Batch(2 * h + p, h, p)


def full(ap):
    return ap.bitcast(F32)


def wait(eng, sem, value):
    if isinstance(value, int) and value <= 0:
        return
    eng.wait_ge(sem, value)


def steps(eng, step):
    last = BATCH // 2
    step(batch(0, 0), None, None, None)
    step(batch(0, 1), batch(0, 0), None, None)
    step(batch(1, 0), batch(0, 1), batch(0, 0), None)
    step(batch(1, 1), batch(1, 0), batch(0, 1), batch(0, 0))
    with eng.Fori(1, last - 1) as i:
        step(batch(i + 1, 0), batch(i, 1), batch(i, 0), batch(i - 1, 1))
        step(batch(i + 1, 1), batch(i + 1, 0), batch(i, 1), batch(i, 0))
    step(None, batch(last - 1, 1), batch(last - 1, 0), batch(last - 2, 1))
    step(None, None, batch(last - 1, 1), batch(last - 1, 0))
    step(None, None, None, batch(last - 1, 1))


def adaln_kernel(nc, x, wqT, wkT, wvT, woT, biases, bo, embT, w1T, w2T, cT, wmod, out):
    rows = nc.dram_tensor("token_rows", (TOKENS, ROW), F32, kind="Internal").ap()
    den_dram = nc.dram_tensor("den_rows", (BATCH, HEADS, SEQ), F32, kind="Internal").ap()
    rden_dram = nc.dram_tensor("rden_rows", (BATCH, HEADS, SEQ), F32, kind="Internal").ap()
    q_parts, k_parts = (nc.dram_tensor(f"{c}_parts", (BATCH, PAIRS, 2, PARTS, HD, SEQ), F32,
                                       kind="Internal").ap() for c in "qk")
    mod_dram = nc.dram_tensor("mod_rows", (BATCH, MODS * D), F32, kind="Internal").ap()
    x_tiles = x.rearrange("b (t p) d -> b p t d", p=P)
    out_rows = out.rearrange("b s d -> (b s) d")
    out_tiles = out.rearrange("b (t p) d -> b p t d", p=P)
    row_tiles = rows.rearrange("(b t p) r -> b p t r", p=P, t=TILES)

    ctx = ExitStack()
    with ctx:
        def sb(name, shape, dt=F32):
            return ctx.enter_context(nc.sbuf_tensor(name, shape, dt))

        def sem(name):
            return ctx.enter_context(nc.semaphore(name))

        wq_sb, wk_sb, wv_sb, wo_sb = (sb(f"w{c}_sb", [P, KH, D]) for c in "qkvo")
        emb_sb = sb("emb_sb", [P, KH, EXPERTS])
        bias_in = sb("bias_in", [P, 3, KH])
        bias_p1 = sb("bias_p1", [P, 2, KH])
        neg_b = sb("neg_b", [P, 2, KH])
        bo_row = sb("bo_row", [1, D])
        ident = sb("ident", [P, P])
        same_head = sb("same_head", [P, P])
        head_sum = sb("head_sum", [P, KH, HEADS])
        causal = sb("causal", [P, P])
        causal_bf = sb("causal_bf", [P, P], BF16)
        ones = sb("ones", [P, SEQ])
        ones_bf = sb("ones_bf", [P, P], BF16)
        neg_half = sb("neg_half", [P, TILES])
        iota_p = sb("iota_p", [P, 1])
        iota_128 = sb("iota_128", [P, P], BF16)
        iota_list = sb("iota_list", [P, LISTS])
        iota_exp = sb("iota_exp", [P, EXPERTS])
        slot_base = sb("slot_base", [P, EXPERTS])
        tile_no = sb("tile_no", [P, TILES, 2])
        spare = sb("spare", [P, 64])
        c_sb = sb("c_sb", [P, KH, BATCH])
        c_exp = sb("c_exp", [P, KH, BATCH])
        silu = sb("silu", [P, KH, BATCH])
        mod_T = sb("mod_T", [P, 2, KH, BATCH])
        bo_all = sb("bo_all", [P, D])
        ga_all = [sb(f"ga_all{p}", [P, D]) for p in range(2)]
        mod_all = [sb(f"mod_all{p}", [P, 3, D]) for p in range(2)]
        x_sb = [sb(f"x_sb{p}", [P, TILES, D]) for p in range(2)]
        stat1 = sb("stat1", [P, TILES, 6])
        mv1 = sb("mv1", [P, TILES, 2])
        rstd1 = sb("rstd1", [P, TILES])
        var1 = sb("var1", [P, TILES])
        negm1 = sb("negm1", [P, TILES])
        xn = sb("xn", [P, TILES, D])
        den_flat = sb("den_flat", [P, HEADS * SEQ // P])
        rden_flat = sb("rden_flat", [P, HEADS * SEQ // P])
        state = [sb(f"state{r}", [P, KH, P]) for r in range(2)]
        oT = [sb(f"oT{r}", [P, KH, P]) for r in range(2)]
        wog = sb("wog", [P, KH, D])
        bo_g = sb("bo_g", [P, D])
        x1 = [sb(f"x1_{p}", [P, TILES, D]) for p in range(2)]
        stat2 = sb("stat2", [P, TILES, 6])
        mv2 = sb("mv2", [P, TILES, 2])
        var2 = sb("var2", [P, TILES])
        rstd2 = sb("rstd2", [P, TILES])
        h2 = sb("h2", [P, TILES, D + EXPERTS])
        h2T = sb("h2T", [P, KH, SEQ])
        logits = sb("logits", [P, TILES, EXPERTS])
        top = sb("top", [P, TILES, 8])
        top_i = sb("top_i", [P, TILES, 8], U32)
        top_f = sb("top_f", [P, TILES, 2])
        gap = sb("gap", [P, TILES])
        e2 = sb("e2", [P, TILES])
        w12 = sb("w12", [P, 2, TILES])
        wsum = sb("wsum", [P, TILES])
        alive = sb("alive", [P, TILES])
        one_hot = sb("one_hot", [P, 2, TILES, EXPERTS])
        weighted = sb("weighted", [P, 2, TILES, EXPERTS])
        both_bf = sb("both_bf", [P, TILES, EXPERTS], BF16)
        counts = sb("counts", [P, TILES + 1, EXPERTS])
        counts_bf = sb("counts_bf", [P, TILES, EXPERTS], BF16)
        fits = sb("fits", [P, TILES, EXPERTS])
        slot = sb("slot", [P, TILES, EXPERTS])
        chosen = sb("chosen", [P, 2, TILES, EXPERTS])
        slot_f = sb("slot_f", [P, TILES, 2])
        slot_i = sb("slot_i", [P, TILES, 2], I32)
        part_i = sb("part_i", [P, 2, TILES, 2], I32)
        part_f = sb("part_f", [P, 2, TILES, 2])
        in_list = sb("in_list", [P, 2 * TILES, 3, LISTS], BF16)
        in_slot = sb("in_slot", [P, 2 * TILES, P], BF16)
        lists = sb("lists", [P, 3, LISTS])
        tok_f = den_flat[:, 0:2 * LISTS].rearrange("p (a l) -> p a l", a=2)
        tok_i = sb("tok_i", [P, 2, LISTS], I32)
        list_in = [sb(f"list_in{q}", [P, SLOT_TILES], I32) for q in range(2)]
        list_back = [sb(f"list_back{q}", [P, SLOT_TILES], I32) for q in range(2)]
        w_now = [sb(f"w_now{q}", [P, SLOT_TILES]) for q in range(2)]

        first_ctx = ExitStack()

        def first(name, shape, dt=F32):
            return first_ctx.enter_context(nc.sbuf_tensor(name, shape, dt))

        q_st = [first(f"q_st{t}", [STACK, PAIRS, 2, P], F32R) for t in range(TILES)]
        k_st = [first(f"k_st{t}", [STACK, PAIRS, P], F32R) for t in range(TILES)]
        q_hi, q_lo, k_hi, k_lo = (first(f"{c}", [P, KH, SEQ], F32R)
                                  for c in ("q_hi", "q_lo", "k_hi", "k_lo"))
        sT = [first(f"sT{r}", [P, HEADS, P]) for r in range(2)]
        v_pad = [first(f"v_pad{p}", [P, TILES, HEADS // 2, 4, HD]) for p in range(2)]
        h1T = first("h1T", [P, KH, SEQ])
        q_exp = first("q_exp", [P, KH, SEQ])
        k_exp = first("k_exp", [P, KH, SEQ])
        kcum = first("kcum", [P, KH, SEQ])
        qT = [first(f"qT{p}", [P, KH, SEQ]) for p in range(2)]
        kT = first("kT", [P, KH, SEQ])
        k_tok = [first(f"k_tok{p}", [P, TILES - 1, D]) for p in range(2)]
        rden = [first(f"rden{p}", [P, KH, SEQ]) for p in range(2)]
        qk = kcum
        den_sb = k_exp[0:HEADS, 0, :]
        first_ctx.close()

        def pair(name, shape, dt=F32):
            return [sb(f"{name}{q}", shape, dt) for q in range(2)]

        w1_sb, w2_sb = pair("w1_sb", [P, KH, INTER]), pair("w2_sb", [P, IB, D])
        w1_hi, w2_hi = pair("w1_hi", [P, KH, INTER], F32R), pair("w2_hi", [P, IB, D], F32R)
        w1_lo, w2_lo = pair("w1_lo", [P, KH, INTER], F32R), pair("w2_lo", [P, IB, D], F32R)
        xg = pair("xg", [P, SLOT_TILES, ROW])
        aside = pair("aside", [P, SLOT_TILES, EXPERTS + D])
        x_hi, x_lo = pair("x_hi", [P, KH, CAP], F32R), pair("x_lo", [P, KH, CAP], F32R)
        in_hi, in_lo = pair("in_hi", [P, IB, CAP], F32R), pair("in_lo", [P, IB, CAP], F32R)
        y_sb = x1
        wmod_sb = [qT[0], qT[1], kT]

        flat = [sT[r][0:BATCH, :, :].rearrange("b h i -> b (h i)") for r in range(2)]
        mod_sb = flat[0][:, 0:MODS * D].rearrange("b (m d) -> b m d", m=MODS)
        mod_abs = flat[1][:, 0:2 * D].rearrange("b (m d) -> b m d", m=2)
        mod_sign = flat[1][:, 2 * D:4 * D].rearrange("b (m d) -> b m d", m=2)

        bv_wide = sT[1][:, HEADS - KH:HEADS, :]

        bank = [ctx.enter_context(nc.psum_tensor(f"bank{i}", [P, 512], F32)) for i in range(8)]
        ring = bank[0:2]
        sc_bank = bank[2:4]
        oT_bank, kv_bank, wo_bank, rt_bank = bank[4:8]

        names = """
            w_in c_in mod_out ident_on mask_on const_on zero_q zero_v c_neg silu_on mod_mm
            mod_ev gate_on mod_t modT_on bias_on bvw_on bo_mm bo_on
            stats1 mean1 rstd1_on xn_on pe_front h1T_on q_expd q_on k_expd k_on v_on k_tok_on
            kcum_on qk_on den_on rden_on head_on
            q_hi_on q_lo_on k_hi_on k_lo_on sc_on masked oT_mm oT_on kv_mm state_on wo_mm wog_on bog_on xb_on x1_on
            stats2 mean2 rstd2_on h2a_on h2_on pe_route h2T_on logits_on top_on topi_on gap_on e2_on
            small oh_on slots_on lists_on w8_on
            tok_on list_ld back_ld gT_mm x_hi_on x_lo_on m1_mm in_hi_on in_lo_on aside_on w_hi_on w_lo_on w_ld m2_mm y_on scat
        """.split()
        S = {n: sem(n) for n in names}
        den_out, den_in, rden_out = sem("den_out"), sem("den_in"), sem("rden_out")
        rden_in = [sem(f"rden_in{p}") for p in range(2)]
        wmod_in = [sem(f"wmod_in{j}") for j in range(3)]
        x_in = [sem(f"x_in{p}") for p in range(2)]
        ga_in = [sem(f"ga_in{p}") for p in range(2)]
        mod_in = [sem(f"mod_in{p}") for p in range(2)]
        parts_out = sem("parts_out")
        st_in = [sem(f"st_in{t}") for t in range(TILES)]
        x1_out = [sem(f"x1_out{p}") for p in range(2)]
        rows_out = sem("rows_out")
        w1_in = [sem(f"w1_in{q}") for q in range(2)]
        w2_in = [sem(f"w2_in{q}") for q in range(2)]
        gathered = [sem(f"gathered{q}") for q in range(2)]
        SMALL = 31

        held = [0]

        def hold(eng, sem, value):
            wait(eng, sem, value)
            if not isinstance(value, int):
                cell = spare[:, held[0]:held[0] + 1]
                held[0] += 1
                if eng is nc.gpsimd:
                    eng.tensor_tensor(cell, neg_half[:, 0:1], neg_half[:, 0:1], ALU.add)
                else:
                    eng.memset(cell, 0.0)

        block = ctx.enter_context(nc.Block())

        def loads_of(e, q):
            return 16 * (e // 2 + 1) if isinstance(e, int) else (e + 2 - q) * 8

        def tok(t):
            return slice(t * P, (t + 1) * P)

        def wide(ap, shape):
            return ap.to_broadcast(shape)

        @block.sync
        def _(sp):
            sp.dma_start(c_sb[:, :, :], cT.rearrange("(k p) b -> p k b", p=P)).then_inc(S["c_in"], 16)
            for j in range(3):
                sp.dma_start(wmod_sb[j][:, :, :],
                             wmod[:, j * 2 * D:(j + 1) * 2 * D].rearrange("(k p) m -> p k m", p=P))\
                    .then_inc(wmod_in[j], 16)

            def load_weights():
                loads = [(wq_sb, wqT), (wk_sb, wkT), (wv_sb, wvT), (wo_sb, woT), (emb_sb, embT)]
                for to, of in loads:
                    sp.dma_start(to[:, :, :], of.rearrange("(k p) m -> p k m", p=P)).then_inc(S["w_in"], 16)
                sp.dma_start(bias_in[:, :, :], biases).then_inc(S["w_in"], 16)
                sp.dma_start(bo_row[:, :], bo.rearrange("(a d) -> a d", a=1)).then_inc(S["w_in"], 16)

            def load_x(b):
                wait(sp, S["xb_on"], b.n - 1)
                sp.dma_start(x_sb[b.p][:, :, :], x_tiles[b.n]).then_inc(x_in[b.p], 16)

            def load_ga(b):
                wait(sp, S["wog_on"], KH * (b.n - 1))
                sp.dma_start(ga_all[b.p][:, :], mod_dram[b.n, GA * D:(GA + 1) * D].partition_broadcast(P))\
                    .then_inc(ga_in[b.p], 16)

            def load_mod(b):
                wait(sp, rows_out, 32 * (b.n - 1))
                sp.dma_start(mod_all[b.p][:, :, :].rearrange("p m d -> p (m d)"),
                             mod_dram[b.n, SB * D:MODS * D].partition_broadcast(P))\
                    .then_inc(mod_in[b.p], 16)

            def store_parts(b, dram, parts, done):
                wait(sp, S[done], b.n + 1)
                for a, part in enumerate(parts):
                    for k in range(KH):
                        sp.dma_start(dram[b.n, k * QUADS:(k + 1) * QUADS, :, a, :, :].rearrange("g s r t -> (g s) r t"),
                                     full(part[:, k, :])).then_inc(parts_out, 16)

            def load_tiles(b, tiles):
                for t in tiles:
                    if t == 0:
                        wait(sp, parts_out, 16 * 2 * PARTS * KH * (b.n + 1))
                    wait(sp, S["sc_on"], TILES * QUADS * (b.n - 1) + QUADS * (t + 1))
                    sp.dma_start(full(k_st[t][:, :, :]),
                                 k_parts[b.n, :, :, :, :, tok(t)].rearrange("g s a r t -> (s a r) g t"))\
                        .then_inc(st_in[t], 16)
                    for h in range(2):
                        at = slice(h * PARTS * HD, (h + 1) * PARTS * HD)
                        sp.dma_start(full(q_st[t][at, :, h, :]),
                                     q_parts[b.n, :, h, :, :, tok(t)].rearrange("g a r t -> (a r) g t"))\
                            .then_inc(st_in[t], 16)

            def spread_den(b):
                wait(sp, S["den_on"], b.n + 1)
                sp.dma_start(den_dram[b.n], den_sb).then_inc(den_out, 16)
                wait(sp, den_out, 16 * (b.n + 1))
                wait(sp, S["rden_on"], b.n)
                sp.dma_start(den_flat[:, :], den_dram[b.n].rearrange("h (g t) -> (h g) t", g=P // HEADS))\
                    .then_inc(den_in, 16)

            def spread_rden(b):
                wait(sp, S["rden_on"], b.n + 1)
                sp.dma_start(rden_dram[b.n].rearrange("h (g t) -> (h g) t", g=P // HEADS), rden_flat[:, :])\
                    .then_inc(rden_out, 16)
                wait(sp, rden_out, 16 * (b.n + 1))
                for h in range(HPH):
                    sp.dma_start(rden[b.p][HD * h:HD * (h + 1), :, :],
                                 rden_dram[b.n, h:HEADS:HPH, :].partition_broadcast(HD))\
                        .then_inc(rden_in[b.p], 16)

            def load_expert(e, q):
                wait(sp, S["w_lo_on"], 2 * (e - 1) - 1)
                wait(sp, S["gT_mm"], KH * (e - 1))
                sp.dma_start(w1_sb[q][:, :, :], w1T[e].rearrange("(k p) i -> p k i", p=P))\
                    .then_inc(w1_in[q], 16)
                wait(sp, S["w_lo_on"], 2 * (e - 1))
                sp.dma_start(w2_sb[q][:, :, :], w2T[e].rearrange("(k p) d -> p k d", p=P))\
                    .then_inc(w2_in[q], 16)

            def step(early, front, attend, route):
                if attend:
                    spread_rden(attend)
                if early:
                    load_x(early)
                    if isinstance(early.n, int) and early.n == 0:
                        load_weights()
                if route:
                    wait(sp, S["x1_on"], TILES * (route.n + 1))
                    sp.dma_start(out_tiles[route.n], x1[route.p][:, :, :]).then_inc(x1_out[route.p], 16)
                if front:
                    if isinstance(front.n, int) and front.n == 0:
                        wait(sp, S["gate_on"], 4)
                        sp.dma_start(mod_dram, mod_sb[:, :, :].rearrange("b m d -> b (m d)"))\
                            .then_inc(S["mod_out"], 16)
                        wait(sp, S["mod_out"], 16)
                        wait(sp, S["zero_q"], TILES)
                    load_ga(front)
                if attend:
                    load_mod(attend)
                if front:
                    store_parts(front, q_parts, (q_hi, q_lo, q_hi), "q_lo_on")
                    store_parts(front, k_parts, (k_hi, k_hi, k_lo), "k_lo_on")
                    load_tiles(front, range(2))
                if not attend and route:
                    wait(sp, S["sc_on"], TILES * QUADS * BATCH)
                    load_expert(0, 0)
                    load_expert(1, 1)
                if route:
                    wait(sp, S["w8_on"], route.n + 1)
                    sp.dma_start(row_tiles[route.n, :, :, 0:ROW_G], h2[:, :, :]).then_inc(rows_out, 16)
                    sp.dma_start(row_tiles[route.n, :, :, ROW_G:ROW],
                                 mod_all[route.p][:, 2, :].unsqueeze(1).to_broadcast([P, TILES, D]))\
                        .then_inc(rows_out, 16)
                if front:
                    spread_den(front)
                    load_tiles(front, range(2, TILES))

            steps(sp, step)

            with sp.Fori(1, EXPERTS // 2) as i:
                load_expert(2 * i, 0)
                load_expert(2 * i + 1, 1)
            wait(sp, S["scat"], 16 * LISTS)
            for p in range(2):
                wait(sp, x1_out[p], 16 * BATCH // 2)

        @block.gpsimd
        def _(gp):
            gp.memset(ident[:, :], 0.0).then_inc(S["ident_on"], 1)
            gp.memset(causal[:, :], 1.0).then_inc(S["mask_on"], 1)
            gp.memset(same_head[:, :], 1.0).then_inc(S["mask_on"], 1)
            gp.memset(ones[:, :], 1.0).then_inc(S["const_on"], 1)
            gp.memset(neg_half[:, :], -0.5).then_inc(S["const_on"], 1)
            gp.wait_ge(S["ident_on"], 1)
            gp.affine_select(out=ident[:, :], in_=ident[:, :], compare_op=ALU.not_equal, fill=1.0,
                             base=0, pattern=[[-1, P]], channel_multiplier=1).then_inc(S["ident_on"], 1)
            gp.wait_ge(S["mask_on"], 2)
            gp.affine_select(out=causal[:, :], in_=causal[:, :], compare_op=ALU.is_ge, fill=0.0,
                             base=0, pattern=[[1, P]], channel_multiplier=-1).then_inc(S["mask_on"], 1)
            heads = same_head[:, :].rearrange("p (h d) -> p h d", d=HD)
            gp.affine_select(out=heads, in_=heads, compare_op=ALU.is_ge, fill=0.0,
                             base=0, pattern=[[-HD, HPH], [0, HD]], channel_multiplier=1)\
                .then_inc(S["mask_on"], 1)
            gp.wait_ge(S["mask_on"], 4)
            gp.affine_select(out=heads, in_=heads, compare_op=ALU.is_ge, fill=0.0,
                             base=HD - 1, pattern=[[HD, HPH], [0, HD]], channel_multiplier=-1)\
                .then_inc(S["mask_on"], 1)
            exact = dict(allow_small_or_imprecise_dtypes=True)
            gp.iota(iota_p[:, :], [[0, 1]], base=0, channel_multiplier=1, **exact).then_inc(S["const_on"], 1)
            gp.iota(iota_128[:, :], [[1, P]], base=0, channel_multiplier=0, **exact).then_inc(S["const_on"], 1)
            gp.iota(iota_list[:, :], [[1, LISTS]], base=0, channel_multiplier=0, **exact)\
                .then_inc(S["const_on"], 1)
            gp.iota(iota_exp[:, :], [[1, EXPERTS]], base=0, channel_multiplier=0, **exact)\
                .then_inc(S["const_on"], 1)
            gp.iota(slot_base[:, :], [[CAP, EXPERTS]], base=-1 - NO_SLOT, channel_multiplier=0, **exact)\
                .then_inc(S["const_on"], 1)
            gp.iota(tile_no[:, :, :], [[1, TILES], [0, 2]], base=0, channel_multiplier=0, **exact)\
                .then_inc(S["const_on"], 1)
            def norm1(b):
                hold(gp, S["mean1"], TILES * (b.n + 1))
                base = 3 * b.n
                gp.tensor_scalar(var1[:, :], mv1[:, :, 1], EPS, None, ALU.add).then_inc(S["rstd1_on"], 1)
                gp.tensor_scalar(negm1[:, :], mv1[:, :, 0], -1.0, None, ALU.mult).then_inc(S["rstd1_on"], 1)
                wait(gp, S["rstd1_on"], base + 2)
                gp.tensor_tensor(rstd1[:, :], var1[:, :], neg_half[:, :], ALU.pow).then_inc(S["rstd1_on"], 1)
                wait(gp, S["rstd1_on"], base + 3)
                hold(gp, S["pe_front"], 11 * (b.n - 1) + 2)
                for t in range(TILES):
                    gp.tensor_scalar(xn[:, t, :], x_sb[b.p][:, t, :], negm1[:, t:t + 1], rstd1[:, t:t + 1],
                                     ALU.add, ALU.mult).then_inc(S["xn_on"], 1)

            def low_part(b, whole, hi, lo, hi_on, lo_on):
                wait(gp, S[hi_on], b.n + 1)
                gp.tensor_tensor(lo[:, :, :], whole[:, :, :], full(hi[:, :, :]), ALU.subtract)\
                    .then_inc(S[lo_on], 1)

            def q_times_kcum(b):
                for k in range(KH):
                    wait(gp, S["kcum_on"], KH * b.n + k + 1)
                    gp.tensor_tensor(qk[:, k, :], qT[b.p][:, k, :], kcum[:, k, :], ALU.mult)\
                        .then_inc(S["qk_on"], 1)

            def gate_out(b):
                if isinstance(b.n, int) and b.n == 0:
                    wait(gp, S["bo_on"], 1)
                wait(gp, ga_in[b.p], 16 * (b.h + 1))
                gp.tensor_tensor(bo_g[:, :], bo_all[:, :], ga_all[b.p][:, :], ALU.mult)\
                    .then_inc(S["bog_on"], 1)
                wait(gp, S["bog_on"], b.n + 1)
                wait(gp, S["h2a_on"], TILES * (b.n - 1))
                wait(gp, x1_out[b.p], 16 * b.h)
                gp.tensor_tensor(x1[b.p][:, :, :], x_sb[b.p][:, :, :],
                                 bo_g[:, :].unsqueeze(1).to_broadcast([P, TILES, D]), ALU.add)\
                    .then_inc(S["xb_on"], 1)
                wait(gp, S["wo_mm"], TILES * b.n)
                for k in range(KH):
                    gp.tensor_tensor(wog[:, k, :], wo_sb[:, k, :], ga_all[b.p][:, :], ALU.mult)\
                        .then_inc(S["wog_on"], 1)

            def norm2(b):
                hold(gp, S["mean2"], TILES * (b.n + 1))
                gp.tensor_scalar(var2[:, :], mv2[:, :, 1], EPS, None, ALU.add).then_inc(S["rstd2_on"], 1)
                wait(gp, S["rstd2_on"], 2 * b.n + 1)
                gp.tensor_tensor(rstd2[:, :], var2[:, :], neg_half[:, :], ALU.pow).then_inc(S["rstd2_on"], 1)

            def step(early, front, attend, route):
                if attend:
                    gate_out(attend)
                if route:
                    norm2(route)
                if front:
                    low_part(front, qT[front.p], q_hi, q_lo, "q_hi_on", "q_lo_on")
                    q_times_kcum(front)
                    low_part(front, kT, k_hi, k_lo, "k_hi_on", "k_lo_on")
                if early:
                    norm1(early)
                    if isinstance(early.n, int) and early.n == 0:
                        for t in range(TILES):
                            gp.memset(full(q_st[t][:, :, :, :]), 0.0).then_inc(S["zero_q"], 1)

            steps(gp, step)

            def gather(e, q):
                wait(gp, S["gT_mm"], KH * (e - 1))
                wait(gp, S["aside_on"], e - 1)
                gp.tensor_copy(list_in[q][:, :], tok_i[:, 0, bass.ds(SLOT_TILES * e, SLOT_TILES)])\
                    .then_inc(S["list_ld"], 1)
                hold(gp, S["list_ld"], e + 1)
                for t in range(SLOT_TILES):
                    gp.indirect_dma_start(
                        out=xg[q][:, t, :], out_offset=None, in_=rows,
                        in_offset=bass.IndirectOffsetOnAxis(ap=list_in[q][:, t:t + 1], axis=0),
                        bounds_check=TOKENS - 1, oob_is_err=False).then_inc(gathered[q], 16)

            def scatter(e, q):
                wait(gp, S["scat"], 16 * SLOT_TILES * e)
                gp.tensor_copy(list_back[q][:, :], tok_i[:, 1, bass.ds(SLOT_TILES * e, SLOT_TILES)])\
                    .then_inc(S["back_ld"], 1)
                hold(gp, S["back_ld"], e + 1)
                for t in range(SLOT_TILES):
                    hold(gp, S["y_on"], SLOT_TILES * e + t + 1)
                    gp.indirect_dma_start(
                        out=out_rows,
                        out_offset=bass.IndirectOffsetOnAxis(ap=list_back[q][:, t:t + 1], axis=0),
                        in_=y_sb[q][:, t, :], in_offset=None,
                        bounds_check=TOKENS - 1, oob_is_err=False, compute_op=ALU.add)\
                        .then_inc(S["scat"], 16)

            wait(gp, S["tok_on"], 4)
            wait(gp, rows_out, 32 * BATCH)
            for p in range(2):
                wait(gp, x1_out[p], 16 * BATCH // 2)
            for e in range(4):
                gather(e, e % 2)
            scatter(0, 0)
            with gp.Fori(1, EXPERTS // 2 - 1) as i:
                gather(2 * i + 2, 0)
                scatter(2 * i - 1, 1)
                gather(2 * i + 3, 1)
                scatter(2 * i, 0)
            for e in range(EXPERTS - 3, EXPERTS):
                scatter(e, e % 2)

        @block.scalar
        def _(act):
            act.wait_ge(S["c_in"], 16)
            act.activation(c_exp[:, :, :], c_sb[:, :, :], ACT.Exp, scale=-1.0).then_inc(S["c_neg"], 1)

            def front_h(b):
                for k in range(KH):
                    wait(act, S["pe_front"], 11 * b.n + k + 1)
                    act.activation(h1T[:, k, :], ring[k][:, :], ACT.Identity,
                                   bias=mod_T[:, 0, k, bass.ds(b.n, 1)],
                                   scale=mod_T[:, 1, k, bass.ds(b.n, 1)]).then_inc(S["h1T_on"], 1)

            def exp_min(w, out, k, done, count):
                act.activation(out[:, k, :], ring[k][:, :], ACT.Relu, bias=neg_b[:, w, k:k + 1],
                               scale=-1.0).then_inc(S[done], 1)
                wait(act, S[done], count + 2 * k + 1)
                act.activation(out[:, k, :], out[:, k, :], ACT.Exp, scale=-1.0).then_inc(S[done], 1)

            def front_exp_q(b):
                for k in range(KH):
                    wait(act, S["pe_front"], 11 * b.n + 3 + k)
                    exp_min(0, q_exp, k, "q_expd", 2 * KH * b.n)

            def front_exp_k(b):
                wait(act, den_out, 16 * b.n)
                for k in range(KH):
                    wait(act, S["pe_front"], 11 * b.n + 5 + k)
                    exp_min(1, k_exp, k, "k_expd", 2 * KH * b.n)

            def high_part(b, whole, hi, whole_on, hi_on):
                wait(act, S[whole_on], KH * (b.n + 1))
                wait(act, parts_out, 16 * 2 * PARTS * KH * b.n)
                act.activation(hi[:, :, :], whole[:, :, :], ACT.Copy).then_inc(S[hi_on], 1)

            def front_v(b):
                for r in range(2):
                    wait(act, S["pe_front"], 11 * b.n + 7 + r)
                    for t in range(2):
                        act.activation(v_pad[b.p][:, 2 * r + t, :, 0:4:3, :],
                                       ring[r][:, t * D:(t + 1) * D]
                                       .rearrange("p (a b c) -> p a b c", b=2, c=HD), ACT.Copy)\
                            .then_inc(S["v_on"], 1)

            def front_kt(b):
                for r in range(2):
                    wait(act, S["pe_front"], 11 * b.n + 9 + r)
                    n = 2 if r == 0 else TILES - 3
                    act.activation(k_tok[b.p][:, 2 * r:2 * r + n, :],
                                   ring[r][:, 0:n * D].rearrange("p (t d) -> p t d", d=D), ACT.Copy)\
                        .then_inc(S["k_tok_on"], 1)

            def front_den(b):
                wait(act, S["pe_front"], 11 * b.n + 11)
                wait(act, S["k_on"], KH * (b.n + 1))
                act.activation(den_sb, ring[0][0:HEADS, :], ACT.Copy).then_inc(S["den_on"], 1)

            def route_h(b, k):
                wait(act, S["pe_route"], 5 * b.n + k + 1)
                act.activation(h2T[:, k, :], rt_bank[:, :], ACT.Copy).then_inc(S["h2T_on"], 1)

            def route_e(b):
                wait(act, S["gap_on"], b.n + 1)
                act.activation(e2[:, :], gap[:, :], ACT.Exp).then_inc(S["e2_on"], 1)

            def step(early, front, attend, route):
                if front:
                    if isinstance(front.n, int) and front.n == 0:
                        wait(act, S["modT_on"], 1)
                        wait(act, S["bias_on"], 2)
                        wait(act, S["zero_v"], 2)
                    front_h(front)
                    front_exp_q(front)
                    high_part(front, qT[front.p], q_hi, "q_on", "q_hi_on")
                    front_exp_k(front)
                if route:
                    route_h(route, 0)
                    route_h(route, 1)
                if front:
                    high_part(front, kT, k_hi, "k_on", "k_hi_on")
                if route:
                    route_e(route)
                if front:
                    front_v(front)
                    front_kt(front)
                    front_den(front)

            steps(act, step)

            def turn_rows(e, q):
                for k in range(KH):
                    wait(act, S["gT_mm"], KH * e + k + 1)
                    act.activation(x_hi[q][:, k, :], bank[k][:, :], ACT.Copy)\
                        .then_inc(S["x_hi_on"], 1)
                wait(act, S["y_on"], SLOT_TILES * (e - 1))
                act.activation(aside[q][:, :, :], xg[q][:, :, ROW_W:ROW], ACT.Copy).then_inc(S["aside_on"], 1)

            def weights_hi(e, q):
                wait(act, S["m2_mm"], SLOT_TILES * (e - 1))
                wait(act, w1_in[q], loads_of(e, q))
                act.activation(w1_hi[q][:, :, :], w1_sb[q][:, :, :], ACT.Copy).then_inc(S["w_hi_on"], 1)
                wait(act, w2_in[q], loads_of(e, q))
                act.activation(w2_hi[q][:, :, :], w2_sb[q][:, :, :], ACT.Copy).then_inc(S["w_hi_on"], 1)

            def relu(e, q):
                for i in range(IB):
                    wait(act, S["m1_mm"], IB * e + i + 1)
                    act.activation(in_hi[q][:, i, :], bank[2 + i][:, :], ACT.Relu)\
                        .then_inc(S["in_hi_on"], 1)

            def next_expert(e, q):
                relu(e, q)
                turn_rows(e + 1, 1 - q)
                weights_hi(e + 1, 1 - q)

            weights_hi(0, 0)
            turn_rows(0, 0)
            next_expert(0, 0)
            next_expert(1, 1)
            with act.Fori(1, EXPERTS // 2 - 1) as i:
                next_expert(2 * i, 0)
                next_expert(2 * i + 1, 1)
            next_expert(EXPERTS - 2, 0)
            relu(EXPERTS - 1, 1)

        @block.tensor
        def _(pe):
            mm = nc.tensor.matmul
            pe.wait_ge(S["silu_on"], 3)

            def modulate(j):
                pe.wait_ge(wmod_in[j], 16)
                for k in range(KH):
                    last = mm(bank[4 + j][0:BATCH, :], silu[:, k, :], wmod_sb[j][:, k, :],
                              start=(k == 0), stop=(k == KH - 1))
                last.then_inc(S["mod_mm"], 1)
            modulate(0)
            modulate(1)
            pe.wait_ge(S["ident_on"], 2)
            pe.wait_ge(S["mod_ev"], 2)
            for j in range(2):
                for k in range(KH):
                    last = nc.tensor.transpose(bank[3][:, (j * KH + k) * BATCH:(j * KH + k + 1) * BATCH],
                                               mod_sb[:, j, k * P:(k + 1) * P], ident[0:BATCH, 0:BATCH])
            last.then_inc(S["mod_t"], 1)
            modulate(2)
            pe.wait_ge(S["bvw_on"], KH)
            pe.wait_ge(S["w_in"], 16 * 7)
            pe.wait_ge(S["const_on"], 2)
            for k in range(KH):
                mm(bank[2][:, 0:D], bv_wide[:, k, :], wo_sb[:, k, :], start=(k == 0), stop=False)
            mm(bank[2][:, 0:D], ones[0:1, 0:P], bo_row[:, :], start=False, stop=True).then_inc(S["bo_mm"], 1)
            pe.wait_ge(S["mask_on"], 5)
            pe.wait_ge(S["head_on"], 3)

            def front_h(b):
                wait(pe, S["xn_on"], TILES * (b.n + 1))
                for k in range(KH):
                    if k == 0:
                        wait(pe, S["den_on"], b.n)
                    else:
                        wait(pe, S["k_tok_on"], 2 * b.n)
                    for t in range(TILES):
                        last = nc.tensor.transpose(ring[k][:, tok(t)], xn[:, t, k * P:(k + 1) * P],
                                                   ident[:, :])
                    last.then_inc(S["pe_front"], 1)

            def project(w, b, m):
                for k in range(KH):
                    last = mm(ring[m][:, :], w[:, k, m * P:(m + 1) * P], h1T[:, k, :],
                              start=(k == 0), stop=(k == KH - 1))
                last.then_inc(S["pe_front"], 1)

            def front_q(b, m):
                wait(pe, S["h1T_on"], KH * (b.n + 1))
                project(wq_sb, b, m)

            def front_k(b, m):
                wait(pe, S["q_on"], KH * b.n + m + 1)
                project(wk_sb, b, m)

            def front_v(b):
                for r in range(2):
                    wait(pe, S["k_on"], KH * b.n + r + 1)
                    for t in range(2):
                        for k in range(KH):
                            last = mm(ring[r][:, t * D:(t + 1) * D], h1T[:, k, tok(2 * r + t)],
                                      wv_sb[:, k, :], start=(k == 0), stop=(k == KH - 1))
                    last.then_inc(S["pe_front"], 1)

            def front_kt(b):
                wait(pe, S["k_on"], KH * (b.n + 1))
                for r in range(2):
                    wait(pe, S["v_on"], 4 * b.n + 2 * r + 2)
                    for t in range(2 if r == 0 else TILES - 3):
                        for k in range(KH):
                            last = nc.tensor.transpose(ring[r][:, t * D + k * P:t * D + (k + 1) * P],
                                                       kT[:, k, tok(2 * r + t)], ident[:, :])
                    last.then_inc(S["pe_front"], 1)

            def front_den(b):
                wait(pe, S["k_tok_on"], 2 * b.n + 1)
                wait(pe, S["qk_on"], KH * (b.n + 1))
                for k in range(KH):
                    last = mm(ring[0][0:HEADS, :], head_sum[:, k, :], qk[:, k, :], start=(k == 0),
                              stop=(k == KH - 1))
                last.then_inc(S["pe_front"], 1)

            def scores(b, t, quads):
                for g in quads:
                    if g == 0:
                        wait(pe, st_in[t], 16 * 3 * (b.n + 1))
                    wait(pe, S["masked"], TILES * QUADS * b.n + QUADS * t + g - 1)
                    for j in range(2):
                        pair = 2 * g + j
                        last = mm(sc_bank[g % 2][:, 2 * j * P:2 * (j + 1) * P].rearrange("p (h i) -> p h i", h=2),
                                  k_st[t][:, pair, :], q_st[t][:, pair, :, :], start=True, stop=True)
                    last.then_inc(S["sc_on"], 1)

            def numerator(b, t):
                wait(pe, S["masked"], QUADS * (TILES * b.n + t + 1))
                wait(pe, S["oT_on"], TILES * b.n + t)
                if t == 0:
                    wait(pe, S["v_on"], 4 * (b.n + 1))
                else:
                    wait(pe, S["state_on"], (TILES - 1) * b.n + t)
                    for k in range(KH):
                        mm(oT_bank[:, k * P:(k + 1) * P], state[(t - 1) % 2][:, k, :], qT[b.p][:, k, tok(t)],
                           start=True, stop=False, skip_group_check=True)
                        heads_of(b, t, k)
                    return
                for k in range(KH):
                    heads_of(b, t, k)

            def heads_of(b, t, k):
                for h in range(HPH):
                    head = k * HPH + h
                    at = 32 * (h // 2)
                    pair = v_pad[b.p][:, t, head // 2, :, :].rearrange("p a b -> p (a b)")
                    last = mm(oT_bank[at:at + 32, k * P:(k + 1) * P], pair[:, 32 * (h % 2):32 * (h % 2) + 32],
                              sT[t % 2][:, head, :], start=(t == 0 and h % 2 == 0), stop=(h % 2 == 1),
                              skip_group_check=True)
                if k == KH - 1:
                    last.then_inc(S["oT_mm"], 1)

            def update_state(b, t):
                if t == 0:
                    wait(pe, S["k_tok_on"], 2 * (b.n + 1))
                    wait(pe, S["v_on"], 4 * (b.n + 1))
                wait(pe, S["state_on"], (TILES - 1) * b.n + t)
                for k in range(KH):
                    last = mm(kv_bank[:, k * P:(k + 1) * P].rearrange("p (a b c) -> p a b c", b=2, c=HD),
                              k_tok[b.p][:, t, k * P:(k + 1) * P],
                              v_pad[b.p][:, t, k * HPH // 2:(k + 1) * HPH // 2, 0:4:3, :],
                              start=(t == 0 and k == 0), stop=(t == TILES - 2), skip_group_check=True)
                last.then_inc(S["kv_mm"], 1)

            def out_project(b, t):
                wait(pe, S["oT_on"], TILES * b.n + t + 1)
                wait(pe, S["wog_on"], KH * (b.n + 1))
                wait(pe, S["x1_on"], TILES * b.n + t)
                for k in range(KH):
                    last = mm(wo_bank[:, 0:D], oT[t % 2][:, k, :], wog[:, k, :], start=(k == 0),
                              stop=(k == KH - 1))
                last.then_inc(S["wo_mm"], 1)

            def route_h(b, k):
                wait(pe, S["h2_on"], TILES * (b.n + 1))
                if k == 0:
                    wait(pe, S["lists_on"], b.n)
                else:
                    wait(pe, S["h2T_on"], KH * b.n + k)
                for t in range(TILES):
                    last = nc.tensor.transpose(rt_bank[:, tok(t)], h2[:, t, k * P:(k + 1) * P],
                                               ident[:, :])
                last.then_inc(S["pe_route"], 1)

            def route_logits(b):
                wait(pe, S["h2T_on"], KH * (b.n + 1))
                for t in range(TILES):
                    for k in range(KH):
                        last = mm(rt_bank[:, t * EXPERTS:(t + 1) * EXPERTS], h2T[:, k, tok(t)],
                                  emb_sb[:, k, :], start=(k == 0), stop=(k == KH - 1))
                last.then_inc(S["pe_route"], 1)

            def route_counts(b):
                wait(pe, S["oh_on"], b.n + 1)
                wait(pe, S["logits_on"], b.n + 1)
                n = TILES * EXPERTS
                mm(rt_bank[:, 0:n], causal_bf[:, :], both_bf[:, :, :].rearrange("p t e -> p (t e)"),
                   start=True, stop=False)
                mm(rt_bank[:, 0:n], ones_bf[:, :], counts_bf[:, :, :].rearrange("p t e -> p (t e)"),
                   start=False, stop=True).then_inc(S["pe_route"], 1)

            def route_lists(b):
                wait(pe, S["slots_on"], b.n + 1)
                for c in range(2 * TILES):
                    last = mm(rt_bank[:, 0:3 * LISTS], in_slot[:, c, :],
                              in_list[:, c, :, :].rearrange("p a l -> p (a l)"), start=(c == 0),
                              stop=(c == 2 * TILES - 1))
                last.then_inc(S["pe_route"], 1)

            def step(early, front, attend, route):
                if front:
                    front_h(front)
                if attend:
                    scores(attend, 0, range(2))
                if route:
                    out_project(route, 3)
                if attend:
                    scores(attend, 0, range(2, QUADS))
                if front:
                    front_q(front, 0)
                if attend:
                    update_state(attend, 0)
                if front:
                    front_q(front, 1)
                if attend:
                    scores(attend, 1, range(2))
                    numerator(attend, 0)
                    scores(attend, 1, range(2, QUADS))
                if front:
                    front_k(front, 0)
                    front_k(front, 1)
                if route:
                    route_h(route, 0)
                if attend:
                    out_project(attend, 0)
                if route:
                    route_h(route, 1)
                if attend:
                    update_state(attend, 1)
                    scores(attend, 2, range(2))
                if route:
                    route_logits(route)
                if attend:
                    scores(attend, 2, range(2, QUADS))
                    numerator(attend, 1)
                if front:
                    front_v(front)
                if attend:
                    scores(attend, 3, range(2))
                    out_project(attend, 1)
                    update_state(attend, 2)
                if front:
                    front_kt(front)
                if attend:
                    scores(attend, 3, range(2, QUADS))
                if front:
                    front_den(front)
                if route:
                    route_counts(route)
                if attend:
                    numerator(attend, 2)
                    out_project(attend, 2)
                    numerator(attend, 3)
                if route:
                    route_lists(route)

            steps(pe, step)

            def product(out, a, b, first, last):
                (a_hi, a_lo), (b_hi, b_lo) = a, b
                mm(out, a_hi, b_hi, start=first, stop=False)
                mm(out, a_lo, b_hi, start=False, stop=False)
                return mm(out, a_hi, b_lo, start=False, stop=last)

            def turn_rows(e, q):
                wait(pe, gathered[q], SLOT_TILES * loads_of(e, q))
                for k in range(KH):
                    wait(pe, S["x_lo_on"], KH * (e - 1) + k + 1)
                    for t in range(SLOT_TILES):
                        last = nc.tensor.transpose(bank[k][:, tok(t)], xg[q][:, t, k * P:(k + 1) * P],
                                                   ident[:, :])
                    last.then_inc(S["gT_mm"], 1)

            def up(e, q):
                wait(pe, S["x_lo_on"], KH * (e + 1))
                wait(pe, S["w_lo_on"], 2 * e + 1)
                for i in range(IB):
                    wait(pe, S["in_lo_on"], IB * (e - 1) + i + 1)
                    cols = slice(i * P, (i + 1) * P)
                    for k in range(KH):
                        last = product(bank[2 + i][:, :], (w1_hi[q][:, k, cols], w1_lo[q][:, k, cols]),
                                       (x_hi[q][:, k, :], x_lo[q][:, k, :]), k == 0, k == KH - 1)
                    last.then_inc(S["m1_mm"], 1)

            def down(e, q):
                wait(pe, S["in_lo_on"], IB * (e + 1))
                wait(pe, S["w_lo_on"], 2 * e + 2)
                for t in range(SLOT_TILES):
                    wait(pe, S["y_on"], SLOT_TILES * e + t - 1)
                    for i in range(IB):
                        last = product(bank[6 + t % 2][:, 0:D], (in_hi[q][:, i, tok(t)], in_lo[q][:, i, tok(t)]),
                                       (w2_hi[q][:, i, :], w2_lo[q][:, i, :]), i == 0, i == IB - 1)
                    last.then_inc(S["m2_mm"], 1)

            wait(pe, S["lists_on"], BATCH)
            turn_rows(0, 0)
            up(0, 0)
            turn_rows(1, 1)
            down(0, 0)
            with pe.Fori(1, EXPERTS // 2) as i:
                up(2 * i - 1, 1)
                turn_rows(2 * i, 0)
                down(2 * i - 1, 1)
                up(2 * i, 0)
                turn_rows(2 * i + 1, 1)
                down(2 * i, 0)
            up(EXPERTS - 1, 1)
            down(EXPERTS - 1, 1)

        @block.vector
        def _(dve):
            v = nc.vector
            v.memset(v_pad[0][:, :, :, :, :], 0.0).then_inc(S["zero_v"], 1)
            dve.wait_ge(S["c_neg"], 1)
            v.tensor_scalar(c_exp[:, :, :], c_exp[:, :, :], 1.0, None, ALU.add).then_inc(S["silu_on"], 1)
            dve.wait_ge(S["silu_on"], 1)
            v.reciprocal(c_exp[:, :, :], c_exp[:, :, :]).then_inc(S["silu_on"], 1)
            dve.wait_ge(S["silu_on"], 2)
            v.tensor_tensor(silu[:, :, :], c_sb[:, :, :], c_exp[:, :, :], ALU.mult).then_inc(S["silu_on"], 1)
            v.memset(v_pad[1][:, :, :, :, :], 0.0).then_inc(S["zero_v"], 1)
            v.memset(ones_bf[:, :], 1.0)
            v.memset(counts[:, :, :], 0.0)
            v.memset(lists[:, :, :], 0.0)
            v.memset(head_sum[:, :, :], 0.0).then_inc(S["head_on"], 1)
            dve.wait_ge(S["mask_on"], 5)
            dve.wait_ge(S["const_on"], 8)
            v.tensor_copy(causal_bf[:, :], causal[:, :])
            dve.wait_ge(S["head_on"], 1)
            for k in range(KH):
                v.tensor_copy(head_sum[:, k, k * HPH:(k + 1) * HPH], same_head[:, 0:P:HD])\
                    .then_inc(S["head_on"], 1)

            def setup():
                for j in range(3):
                    dve.wait_ge(S["mod_mm"], j + 1)
                    v.tensor_copy(mod_sb[:, 2 * j:2 * j + 2, :],
                                  bank[4 + j][0:BATCH, :].rearrange("b (m d) -> b m d", m=2))\
                        .then_inc(S["mod_ev"], 1)
                    if j == 0:
                        dve.wait_ge(S["mod_ev"], 1)
                        v.tensor_scalar(mod_sb[:, CA, :], mod_sb[:, CA, :], 1.0, None, ALU.add)\
                            .then_inc(S["mod_ev"], 1)
                        dve.wait_ge(S["w_in"], 16 * 7)
                        v.tensor_scalar(bias_p1[:, :, :], bias_in[:, 0:2, :], 1.0, None, ALU.add)\
                            .then_inc(S["bias_on"], 1)
                        v.tensor_scalar(neg_b[:, :, :], bias_in[:, 0:2, :], -1.0, None, ALU.mult)\
                            .then_inc(S["bias_on"], 1)
                        for k in range(KH):
                            v.tensor_scalar(bv_wide[:, k, :], ones[:, 0:P], bias_in[:, 2, k:k + 1], None,
                                            ALU.mult).then_inc(S["bvw_on"], 1)
                        dve.wait_ge(S["mod_t"], 1)
                        v.tensor_copy(mod_T[:, :, :, :],
                                      bank[3][:, 0:2 * KH * BATCH]
                                      .rearrange("p (j k b) -> p j k b", j=2, k=KH)).then_inc(S["modT_on"], 1)
                dve.wait_ge(S["mod_ev"], 4)
                v.tensor_scalar(mod_sb[:, CB, :], mod_sb[:, CB, :], 1.0, None, ALU.add)\
                    .then_inc(S["gate_on"], 1)
                gates = mod_sb[:, GA:MODS:GB - GA, :]
                v.scalar_tensor_tensor(out=mod_abs[:, :, :], in0=gates, scalar=-1.0, in1=gates,
                                       op0=ALU.mult, op1=ALU.max).then_inc(S["gate_on"], 1)
                v.tensor_scalar(mod_sign[:, :, :], gates, 0.0, 2.0, ALU.is_ge, ALU.mult)\
                    .then_inc(S["gate_on"], 1)
                dve.wait_ge(S["gate_on"], 3)
                v.tensor_scalar(mod_abs[:, :, :], mod_abs[:, :, :], 0.25, None, ALU.max)\
                    .then_inc(S["bias_on"], 1)
                dve.wait_ge(S["bias_on"], 3)
                v.scalar_tensor_tensor(out=gates, in0=mod_sign[:, :, :], scalar=-1.0, in1=mod_abs[:, :, :],
                                       op0=ALU.add, op1=ALU.mult).then_inc(S["gate_on"], 1)
                dve.wait_ge(S["bo_mm"], 1)
                v.tensor_copy(bo_all[:, :], bank[2][:, 0:D]).then_inc(S["bo_on"], 1)

            def early_stats(b):
                wait(dve, x_in[b.p], 16 * (b.h + 1))
                for t in range(TILES):
                    v.bn_stats(stat1[:, t, :], x_sb[b.p][:, t, :]).then_inc(S["stats1"], 1)
                hold(dve, S["stats1"], TILES * (b.n + 1))
                for t in range(TILES):
                    v.bn_aggr(mv1[:, t, :], stat1[:, t, :]).then_inc(S["mean1"], 1)

            def q_max(b, k):
                wait(dve, S["q_expd"], 2 * KH * b.n + 2 * k + 2)
                v.scalar_tensor_tensor(out=qT[b.p][:, k, :], in0=ring[k][:, :], scalar=bias_p1[:, 0, k:k + 1],
                                       in1=q_exp[:, k, :], op0=ALU.add, op1=ALU.max).then_inc(S["q_on"], 1)

            def front_k(b):
                for k in range(KH):
                    wait(dve, S["k_expd"], 2 * KH * b.n + 2 * k + 2)
                    v.scalar_tensor_tensor(out=kT[:, k, :], in0=ring[k][:, :],
                                           scalar=bias_p1[:, 1, k:k + 1], in1=k_exp[:, k, :],
                                           op0=ALU.add, op1=ALU.max).then_inc(S["k_on"], 1)
                for k in range(KH):
                    wait(dve, S["k_on"], KH * b.n + k + 1)
                    v.tensor_tensor_scan(kcum[:, k, :], ones[:, :], kT[:, k, :], 0.0,
                                         ALU.mult, ALU.add).then_inc(S["kcum_on"], 1)

            def invert_den(b):
                wait(dve, den_in, 16 * (b.n + 1))
                wait(dve, rden_out, 16 * b.n)
                v.reciprocal(rden_flat[:, :], den_flat[:, :]).then_inc(S["rden_on"], 1)

            def normalise(b, t):
                if t == 0:
                    wait(dve, rden_in[b.p], 16 * HPH * (b.h + 1))
                wait(dve, S["oT_mm"], TILES * b.n + t + 1)
                wait(dve, S["wo_mm"], TILES * b.n + t - 1)
                v.tensor_tensor(oT[t % 2][:, :, :], oT_bank[:, 0:KH * P].rearrange("p (k i) -> p k i", k=KH),
                                rden[b.p][:, :, tok(t)], ALU.mult).then_inc(S["oT_on"], 1)

            def mask(b, t, quads):
                for g in quads:
                    use = TILES * QUADS * b.n + QUADS * t + g
                    if g == 0:
                        wait(dve, S["oT_mm"], TILES * b.n + t - 1)
                    wait(dve, S["sc_on"], use + 1)
                    v.tensor_tensor(sT[t % 2][:, 4 * g:4 * g + 4, :],
                                    sc_bank[g % 2][:, :].rearrange("p (h i) -> p h i", h=4),
                                    causal[:, :].unsqueeze(1).to_broadcast([P, 4, P]), ALU.mult)\
                        .then_inc(S["masked"], 1)

            def keep_state(b, t):
                wait(dve, S["kv_mm"], (TILES - 1) * b.n + t + 1)
                wait(dve, S["oT_mm"], TILES * b.n + t)
                v.tensor_tensor(state[t % 2][:, :, :],
                                kv_bank[:, 0:KH * P].rearrange("p (k e) -> p k e", k=KH),
                                same_head[:, :].unsqueeze(1).to_broadcast([P, KH, P]), ALU.mult)\
                    .then_inc(S["state_on"], 1)

            def residual(b, t):
                if t == 0:
                    wait(dve, S["xb_on"], b.n + 1)
                wait(dve, S["wo_mm"], TILES * b.n + t + 1)
                v.tensor_tensor(x1[b.p][:, t, :], wo_bank[:, 0:D], x1[b.p][:, t, :], ALU.add)\
                    .then_inc(S["x1_on"], 1)
                wait(dve, S["x1_on"], TILES * b.n + t + 1)
                v.bn_stats(stat2[:, t, :], x1[b.p][:, t, :]).then_inc(S["stats2"], 1)

            def mean2(b):
                hold(dve, S["stats2"], TILES * (b.n + 1))
                for t in range(TILES):
                    v.bn_aggr(mv2[:, t, :], stat2[:, t, :]).then_inc(S["mean2"], 1)

            def route_h(b):
                wait(dve, S["mean2"], TILES * (b.n + 1))
                wait(dve, mod_in[b.p], 16 * (b.h + 1))
                wait(dve, rows_out, 32 * b.n)
                for t in range(TILES):
                    v.scalar_tensor_tensor(out=h2[:, t, 0:D], in0=x1[b.p][:, t, :], scalar=mv2[:, t, 0:1],
                                           in1=mod_all[b.p][:, 1, :], op0=ALU.subtract, op1=ALU.mult)\
                        .then_inc(S["h2a_on"], 1)
                wait(dve, S["rstd2_on"], 2 * (b.n + 1))
                for t in range(TILES):
                    wait(dve, S["h2a_on"], TILES * b.n + t + 1)
                    v.scalar_tensor_tensor(out=h2[:, t, 0:D], in0=h2[:, t, 0:D], scalar=rstd2[:, t:t + 1],
                                           in1=mod_all[b.p][:, 0, :], op0=ALU.mult, op1=ALU.add)\
                        .then_inc(S["h2_on"], 1)

            def chain(b):
                done = [0]

                def mark(ins, sync=True):
                    ins.then_inc(S["small"], 1)
                    done[0] += 1
                    if sync:
                        wait(dve, S["small"], SMALL * b.n + done[0])
                return done, mark

            te = [P, TILES, EXPERTS]

            def route_top(b):
                wait(dve, S["pe_route"], 5 * b.n + 3)
                v.tensor_copy(logits[:, :, :],
                              rt_bank[:, 0:TILES * EXPERTS].rearrange("p (t e) -> p t e", t=TILES))\
                    .then_inc(S["logits_on"], 1)
                hold(dve, S["logits_on"], b.n + 1)
                for t in range(TILES):
                    v.max(top[:, t, :], logits[:, t, :]).then_inc(S["top_on"], 1)
                hold(dve, S["top_on"], TILES * (b.n + 1))
                for t in range(TILES):
                    v.max_index(top_i[:, t, :], top[:, t, :], logits[:, t, :]).then_inc(S["topi_on"], 1)
                v.tensor_tensor(gap[:, :], top[:, :, 1], top[:, :, 0], ALU.subtract).then_inc(S["gap_on"], 1)
                wait(dve, S["topi_on"], TILES * (b.n + 1))

            def route_choose(b, mark):
                mark(v.tensor_copy(top_f[:, :, :], top_i[:, :, 0:2]))
                for j in range(2):
                    mark(v.tensor_tensor(one_hot[:, j, :, :], iota_exp[:, :].unsqueeze(1).to_broadcast(te),
                                         top_f[:, :, j:j + 1].to_broadcast(te), ALU.is_equal), sync=False)
                wait(dve, S["e2_on"], b.n + 1)
                mark(v.tensor_scalar(wsum[:, :], e2[:, :], 1.0, None, ALU.add))
                mark(v.reciprocal(w12[:, 0, :], wsum[:, :]))
                mark(v.tensor_tensor(w12[:, 1, :], e2[:, :], w12[:, 0, :], ALU.mult))
                mark(v.tensor_scalar(alive[:, :], w12[:, 1, :], 0.0, None, ALU.is_gt))
                mark(v.tensor_tensor(one_hot[:, 1, :, :], one_hot[:, 1, :, :],
                                     alive[:, :].unsqueeze(2).to_broadcast(te), ALU.mult))
                mark(v.tensor_tensor(both_bf[:, :, :], one_hot[:, 0, :, :], one_hot[:, 1, :, :], ALU.add))
                for t in range(TILES):
                    mark(v.tensor_tensor(counts[:, t + 1, :], counts[:, t, :], both_bf[:, t, :], ALU.add))
                v.tensor_copy(counts_bf[:, :, :], counts[:, 0:TILES, :]).then_inc(S["oh_on"], 1)
                for j in range(2):
                    mark(v.tensor_tensor(weighted[:, j, :, :], one_hot[:, j, :, :],
                                         w12[:, j, :].unsqueeze(2).to_broadcast(te), ALU.mult))
                v.tensor_tensor(h2[:, :, D:D + EXPERTS], weighted[:, 0, :, :], weighted[:, 1, :, :], ALU.add)\
                    .then_inc(S["w8_on"], 1)
                wait(dve, S["oh_on"], b.n + 1)
                mark(v.tensor_copy(counts[:, 0, :], counts[:, TILES, :]))

            def route_slots(b, mark):
                wait(dve, S["pe_route"], 5 * b.n + 4)
                count = rt_bank[:, 0:TILES * EXPERTS].rearrange("p (t e) -> p t e", t=TILES)
                mark(v.tensor_scalar(fits[:, :, :], count, float(CAP), None, ALU.is_le), sync=False)
                mark(v.tensor_tensor(slot[:, :, :], count, slot_base[:, :].unsqueeze(1).to_broadcast(te),
                                     ALU.add))
                mark(v.tensor_tensor(slot[:, :, :], slot[:, :, :], fits[:, :, :], ALU.mult))
                for j in range(2):
                    mark(v.tensor_tensor(chosen[:, j, :, :], one_hot[:, j, :, :], slot[:, :, :], ALU.mult))
                    mark(v.tensor_reduce(slot_f[:, :, j], chosen[:, j, :, :], AX.X, ALU.add))
                mark(v.tensor_scalar(slot_i[:, :, :], slot_f[:, :, :], float(NO_SLOT), None, ALU.add))

            def route_places(b, done, mark):
                mark(v.tensor_scalar(part_i[:, 0, :, :], slot_i[:, :, :], P - 1, None, ALU.bitwise_and),
                     sync=False)
                mark(v.tensor_scalar(part_i[:, 1, :, :], slot_i[:, :, :], 7, None, ALU.arith_shift_right))
                mark(v.tensor_copy(part_f[:, :, :, :], part_i[:, :, :, :]))
                shape = [P, 2 * TILES, LISTS]
                list_no = part_f[:, 1, :, :].rearrange("p t j -> p (t j)").unsqueeze(2).to_broadcast(shape)
                mark(v.tensor_tensor(in_list[:, :, 2, :], iota_list[:, :].unsqueeze(1).to_broadcast(shape),
                                     list_no, ALU.is_equal))
                mark(v.tensor_scalar(in_list[:, :, 1, :], in_list[:, :, 2, :], iota_p[:, 0:1], None, ALU.mult),
                     sync=False)
                mark(v.tensor_tensor(in_list[:, :, 0, :], in_list[:, :, 2, :],
                                     tile_no[:, :, :].rearrange("p t j -> p (t j)").unsqueeze(2)
                                     .to_broadcast(shape), ALU.mult))
                mark(v.tensor_scalar(tile_no[:, :, :], tile_no[:, :, :], float(TILES), None, ALU.add),
                     sync=False)
                for c in range(2 * TILES):
                    ins = v.tensor_scalar(in_slot[:, c, :], iota_128[:, :],
                                          part_f[:, 0, c // 2, c % 2:c % 2 + 1], None, ALU.is_equal)
                ins.then_inc(S["slots_on"], 1)
                assert done[0] == SMALL, done

            def route_lists(b):
                wait(dve, S["pe_route"], 5 * (b.n + 1))
                v.tensor_tensor(lists[:, :, :], rt_bank[:, 0:3 * LISTS].rearrange("p (a l) -> p a l", a=3),
                                lists[:, :, :], ALU.add).then_inc(S["lists_on"], 1)

            def step(early, front, attend, route):
                if attend:
                    mask(attend, 0, range(2))
                if route:
                    residual(route, 3)
                    mean2(route)
                if attend:
                    mask(attend, 0, range(2, QUADS))
                    invert_den(attend)
                if front:
                    if isinstance(front.n, int) and front.n == 0:
                        setup()
                if attend:
                    keep_state(attend, 0)
                if front:
                    q_max(front, 0)
                if attend:
                    mask(attend, 1, range(2))
                if front:
                    q_max(front, 1)
                if attend:
                    mask(attend, 1, range(2, QUADS))
                if route:
                    route_h(route)
                if attend:
                    normalise(attend, 0)
                if front:
                    front_k(front)
                if attend:
                    residual(attend, 0)
                    keep_state(attend, 1)
                    mask(attend, 2, range(2))
                if early:
                    early_stats(early)
                if attend:
                    mask(attend, 2, range(2, QUADS))
                if route:
                    route_top(route)
                if attend:
                    normalise(attend, 1)
                if route:
                    done, mark = chain(route)
                    route_choose(route, mark)
                if attend:
                    mask(attend, 3, range(2))
                    residual(attend, 1)
                    keep_state(attend, 2)
                    mask(attend, 3, range(2, QUADS))
                if route:
                    route_slots(route, mark)
                if attend:
                    normalise(attend, 2)
                if route:
                    route_places(route, done, mark)
                if attend:
                    residual(attend, 2)
                    normalise(attend, 3)
                if route:
                    route_lists(route)

            steps(dve, step)

            dve.wait_ge(S["lists_on"], BATCH)
            v.scalar_tensor_tensor(out=tok_f[:, 0, :], in0=lists[:, 0, :], scalar=float(P), in1=lists[:, 1, :],
                                   op0=ALU.mult, op1=ALU.add).then_inc(S["tok_on"], 1)
            v.tensor_scalar(tok_f[:, 1, :], lists[:, 2, :], -float(TOKENS), float(TOKENS), ALU.mult, ALU.add)\
                .then_inc(S["tok_on"], 1)
            dve.wait_ge(S["tok_on"], 2)
            v.tensor_copy(tok_i[:, 0, :], tok_f[:, 0, :]).then_inc(S["tok_on"], 1)
            v.tensor_tensor(tok_i[:, 1, :], tok_f[:, 1, :], tok_f[:, 0, :], ALU.add).then_inc(S["tok_on"], 1)

            def weights_lo(e, q, w, raw, hi, lo):
                wait(dve, S["w_hi_on"], 2 * e + w + 1)
                v.tensor_tensor(lo[q][:, :, :], raw[q][:, :, :], full(hi[q][:, :, :]), ALU.subtract)\
                    .then_inc(S["w_lo_on"], 1)

            def rows_lo(e, q):
                for k in range(KH):
                    wait(dve, S["x_hi_on"], KH * e + k + 1)
                    v.tensor_tensor(x_lo[q][:, k, :], bank[k][:, :], full(x_hi[q][:, k, :]), ALU.subtract)\
                        .then_inc(S["x_lo_on"], 1)

            def relu_lo(e, q):
                for i in range(IB):
                    wait(dve, S["in_hi_on"], IB * e + i + 1)
                    v.scalar_tensor_tensor(out=in_lo[q][:, i, :], in0=bank[2 + i][:, :], scalar=0.0,
                                           in1=full(in_hi[q][:, i, :]), op0=ALU.max, op1=ALU.subtract)\
                        .then_inc(S["in_lo_on"], 1)

            def weigh(e, q, tiles):
                for t in tiles:
                    if t == 0:
                        wait(dve, S["aside_on"], e + 1)
                        v.tensor_copy(w_now[q][:, :].unsqueeze(2), aside[q][:, :, bass.ds(e, 1)])\
                            .then_inc(S["w_ld"], 1)
                        wait(dve, S["w_ld"], e + 1)
                        wait(dve, S["scat"], 16 * SLOT_TILES * (e - 1))
                    wait(dve, S["m2_mm"], SLOT_TILES * e + t + 1)
                    v.scalar_tensor_tensor(out=y_sb[q][:, t, :], in0=bank[6 + t % 2][:, 0:D],
                                           scalar=w_now[q][:, t:t + 1], in1=aside[q][:, t, EXPERTS:],
                                           op0=ALU.mult, op1=ALU.mult).then_inc(S["y_on"], 1)

            def next_expert(e, q):
                relu_lo(e, q)
                rows_lo(e + 1, 1 - q)
                weigh(e, q, range(2))
                weights_lo(e + 1, 1 - q, 0, w1_sb, w1_hi, w1_lo)
                weigh(e, q, range(2, SLOT_TILES))
                weights_lo(e + 1, 1 - q, 1, w2_sb, w2_hi, w2_lo)

            weights_lo(0, 0, 0, w1_sb, w1_hi, w1_lo)
            weights_lo(0, 0, 1, w2_sb, w2_hi, w2_lo)
            rows_lo(0, 0)
            for p in range(2):
                dve.wait_ge(x1_out[p], 16 * BATCH // 2)
            next_expert(0, 0)
            next_expert(1, 1)
            with dve.Fori(1, EXPERTS // 2 - 1) as i:
                next_expert(2 * i, 0)
                next_expert(2 * i + 1, 1)
            next_expert(EXPERTS - 2, 0)
            relu_lo(EXPERTS - 1, 1)
            weigh(EXPERTS - 1, 1, range(SLOT_TILES))


def kernel(L0_attn_x, L0_attn_Wq, L0_attn_bq, L0_attn_Wk, L0_attn_bk, L0_attn_Wv, L0_attn_bv, L0_attn_Wo,
           L0_attn_bo, L0_ffn_expert_embeddings, L0_ffn_first_linear, L0_ffn_second_linear, L0_c, L0_wmod):
    import numpy as np
    import concourse.bacc as bacc
    from concourse.bass_utils import run_bass_kernel_spmd

    arrays = {
        "x": L0_attn_x,
        "wqT": L0_attn_Wq.T, "wkT": L0_attn_Wk.T, "wvT": L0_attn_Wv.T, "woT": L0_attn_Wo.T,
        "biases": np.stack([L0_attn_bq, L0_attn_bk, L0_attn_bv]).reshape(3, KH, P).transpose(2, 0, 1),
        "bo": L0_attn_bo,
        "embT": L0_ffn_expert_embeddings.T,
        "w1T": L0_ffn_first_linear.transpose(0, 2, 1),
        "w2T": L0_ffn_second_linear.transpose(0, 2, 1),
        "cT": L0_c.T, "wmod": L0_wmod,
    }
    nc = bacc.Bacc("TRN2", target_bir_lowering=False, num_devices=1)
    given, args = {}, []
    for name, a in arrays.items():
        given[name] = np.ascontiguousarray(a)
        args.append(nc.dram_tensor(name, given[name].shape, mybir.dt.from_np(given[name].dtype),
                                   kind="ExternalInput").ap())
    args.append(nc.dram_tensor("out", (BATCH, SEQ, D), F32, kind="ExternalOutput").ap())
    adaln_kernel(nc, *args)
    return run_bass_kernel_spmd(nc, [given], core_ids=[0]).results[0]["out"]
```
